# Optimizing a Trainium2 kernel written in Bass

```python
import numpy as np
import jax
import jax.numpy as jnp

def _softmax(x, axis=-1):
    return jax.nn.softmax(x, axis=axis)

def _gelu(x):
    return jax.nn.gelu(x, approximate=True)

def _silu(x):
    return jax.nn.silu(x)

def _sigmoid(x):
    return jax.nn.sigmoid(x)

def _layernorm(x, axis=-1, eps=1e-05):
    m = jnp.mean(x, axis=axis, keepdims=True)
    v = jnp.var(x, axis=axis, keepdims=True)
    return (x - m) / jnp.sqrt(v + eps)

def _scatter_add(tgt, idx, src, axis=0):
    return tgt.at[idx].add(src)

def _segment_sum(src, seg, n):
    return jax.ops.segment_sum(src, seg, n)
kernel_name = 'mk_early_fusion_d2_tok_img768_r4_e402b5'

def setup_inputs(seed: int=0):
    np.random.seed(seed)
    _w = jnp.asarray

    def _rec_inputs():
        import jax
        import jax.numpy as jnp
        _rk = jax.random.key(seed)
        x = -0.000348323 + 0.999952 * jax.random.normal(jax.random.fold_in(_rk, 1), (8, 3, 96, 96), jnp.float32)
        txt = 0.00108508 + 1.0006 * jax.random.normal(jax.random.fold_in(_rk, 2), (8, 128, 192), jnp.float32)
        return (x, txt)
    x, txt = _rec_inputs()

    def _L0_tok_setup():
        import jax, jax.numpy as jnp
        import numpy as np
        PATCH = 16
        DIM = 192
        LN_EPS = 1e-05

        def _spt_forward(x, ln_gamma, ln_beta, w, b):
            B, C, H, W = x.shape
            p = PATCH
            x_right = jnp.pad(x, ((0, 0), (0, 0), (0, 0), (1, 0)))[:, :, :, :-1]
            x_left = jnp.pad(x, ((0, 0), (0, 0), (0, 0), (0, 1)))[:, :, :, 1:]
            x_down = jnp.pad(x, ((0, 0), (0, 0), (1, 0), (0, 0)))[:, :, :-1, :]
            x_up = jnp.pad(x, ((0, 0), (0, 0), (0, 1), (0, 0)))[:, :, 1:, :]
            xc = jnp.concatenate((x, x_right, x_left, x_down, x_up), axis=1)
            C5 = 5 * C
            h, wgrid = (H // p, W // p)
            tokens = xc.reshape(B, C5, h, p, wgrid, p)
            tokens = tokens.transpose(0, 2, 4, 3, 5, 1)
            tokens = tokens.reshape(B, h * wgrid, p * p * C5)
            mean = jnp.mean(tokens, axis=-1, keepdims=True)
            var = jnp.var(tokens, axis=-1, keepdims=True)
            normed = (tokens - mean) * jax.lax.rsqrt(var + LN_EPS) * ln_gamma + ln_beta
            return jnp.einsum('bnd,de->bne', normed, w) + b
        key = jax.random.key(seed)
        k1, k2 = jax.random.split(key)
        B, C, H, W = (32, 3, 96, 96)
        patch_dim = PATCH * PATCH * 5 * C
        x = jax.random.normal(k1, (B, C, H, W), dtype=jnp.float32)
        ln_gamma = jnp.ones((patch_dim,), dtype=jnp.float32)
        ln_beta = jnp.zeros((patch_dim,), dtype=jnp.float32)
        w = jax.random.normal(k2, (patch_dim, DIM), dtype=jnp.float32) * patch_dim ** (-0.5)
        b = jnp.zeros((DIM,), dtype=jnp.float32)
        return {'x': x, 'ln_gamma': ln_gamma, 'ln_beta': ln_beta, 'w': w, 'b': b}
    _L0_tok_all = _L0_tok_setup()
    _L0_tok_in = {k: v for k, v in _L0_tok_all.items() if k in ('ln_gamma', 'ln_beta', 'w', 'b')}
    del _L0_tok_all

    def _L0_attn_setup():
        import jax, jax.numpy as jnp
        import numpy as np
        from jax import lax
        B_SZ, L, D, N, R = (1, 1024, 192, 16, 48)

        def _soft_clamp(x, lo=0.0001, hi=10.0):
            center = (hi + lo) / 2.0
            half_range = (hi - lo) / 2.0
            return center + half_range * jnp.tanh((x - center) / half_range)
        key = jax.random.key(seed)
        ks = jax.random.split(key, 6)
        x = jax.random.normal(ks[0], (B_SZ, L, D), jnp.float32)
        A_log = jnp.log(jnp.broadcast_to(jnp.arange(1, N + 1, dtype=jnp.float32), (D, N)))
        D_param = jnp.ones((D,), jnp.float32)
        W_bc = jax.random.normal(ks[1], (D, 2 * N), jnp.float32) / np.sqrt(D).astype(np.float32)
        W_dt = jax.random.normal(ks[2], (D, R), jnp.float32) / np.sqrt(D).astype(np.float32)
        W_dtp = jax.random.normal(ks[3], (R, D), jnp.float32) / np.sqrt(R).astype(np.float32)
        dt = jax.random.uniform(ks[4], (D,), jnp.float32, 0.001, 0.1)
        dt = jnp.clip(dt, 0.0001)
        b_dt = dt + jnp.log(-jnp.expm1(-dt))
        rms_scale = jnp.ones((D,), jnp.float32)
        return {'x': x, 'A_log': A_log, 'D_param': D_param, 'W_bc': W_bc, 'W_dt': W_dt, 'W_dtp': W_dtp, 'b_dt': b_dt, 'rms_scale': rms_scale}
    _L0_attn_all = _L0_attn_setup()
    _L0_attn_in = {k: v for k, v in _L0_attn_all.items() if k in ('A_log', 'D_param', 'W_bc', 'W_dt', 'W_dtp', 'b_dt', 'rms_scale')}
    del _L0_attn_all

    def _L0_ffn_setup():
        import jax, jax.numpy as jnp
        import numpy as np
        E = 8
        K = 2
        D = 192
        F = 4 * D
        key = jax.random.key(seed)
        ks = jax.random.split(key, 10)
        s_exp = 0.02
        return {'x': jax.random.normal(ks[0], (4, 256, D), jnp.float32), 'W1': jax.random.normal(ks[1], (E, F, D), jnp.float32) * s_exp, 'b1': jax.random.normal(ks[2], (E, F), jnp.float32) * s_exp, 'W2': jax.random.normal(ks[3], (E, D, F), jnp.float32) * s_exp, 'b2': jax.random.normal(ks[4], (E, D), jnp.float32) * s_exp, 'Wr1': jax.random.normal(ks[5], (D, D), jnp.float32) * s_exp, 'br1': jax.random.normal(ks[6], (D,), jnp.float32) * s_exp, 'Wr2': jax.random.normal(ks[7], (E, D), jnp.float32) * s_exp, 'br2': jax.random.normal(ks[8], (E,), jnp.float32) * s_exp}
    _L0_ffn_all = _L0_ffn_setup()
    _L0_ffn_in = {k: v for k, v in _L0_ffn_all.items() if k in ('W1', 'b1', 'W2', 'b2', 'Wr1', 'br1', 'Wr2', 'br2')}
    del _L0_ffn_all

    def _L1_attn_setup():
        import jax, jax.numpy as jnp
        import numpy as np
        B, N, C = (16, 256, 192)
        NUM_HEADS, BANK = (12, 64)
        HEAD_DIM = C // NUM_HEADS
        LN_EPS = 1e-05

        def _split_heads_bank(bank, b):
            t = jnp.broadcast_to(bank, (b,) + bank.shape)
            return t.reshape(b, BANK, NUM_HEADS, HEAD_DIM).transpose(0, 2, 1, 3)

        def _reference_tuple_inner(x, qkv_w, qkv_b, proj_w, proj_b, norm_w, norm_b, bank_k, bank_v):
            b, n, c = x.shape
            h, d = (NUM_HEADS, HEAD_DIM)
            qkv = jnp.einsum('bnc,fc->bnf', x, qkv_w) + qkv_b
            qkv = qkv.reshape(b, n, 3, h, d).transpose(2, 0, 3, 1, 4)
            q, k, v = (qkv[0], qkv[1], qkv[2])
            k_full = jnp.concatenate([k, _split_heads_bank(bank_k, b)], axis=2)
            v_full = jnp.concatenate([v, _split_heads_bank(bank_v, b)], axis=2)
            scores = jnp.einsum('bhnd,bhmd->bhnm', q, k_full) / jnp.sqrt(jnp.asarray(d, x.dtype))
            attn = jax.nn.softmax(scores, axis=-1)
            out = jnp.einsum('bhnm,bhmd->bhnd', attn, v_full)
            out = out.transpose(0, 2, 1, 3).reshape(b, n, c)
            p = jnp.einsum('bnc,oc->bno', out, proj_w) + proj_b
            mu = jnp.mean(p, axis=-1, keepdims=True)
            var = jnp.mean(jnp.square(p - mu), axis=-1, keepdims=True)
            bank_update = (p - mu) * jax.lax.rsqrt(var + LN_EPS) * norm_w + norm_b
            return (out, bank_update)
        key = jax.random.key(seed)
        ks = jax.random.split(key, 9)
        s = 0.02
        return {'x': jax.random.normal(ks[0], (B, N, C), dtype=jnp.float32), 'qkv_w': jax.random.normal(ks[1], (3 * C, C), dtype=jnp.float32) * s, 'qkv_b': jnp.zeros((3 * C,), dtype=jnp.float32), 'proj_w': jax.random.normal(ks[2], (C, C), dtype=jnp.float32) * s, 'proj_b': jnp.zeros((C,), dtype=jnp.float32), 'norm_w': jnp.ones((C,), dtype=jnp.float32), 'norm_b': jnp.zeros((C,), dtype=jnp.float32), 'bank_k': jax.random.normal(ks[3], (BANK, C), dtype=jnp.float32) * s, 'bank_v': jax.random.normal(ks[4], (BANK, C), dtype=jnp.float32) * s}
    _L1_attn_all = _L1_attn_setup()
    _L1_attn_in = {k: v for k, v in _L1_attn_all.items() if k in ('qkv_w', 'qkv_b', 'proj_w', 'proj_b', 'norm_w', 'norm_b', 'bank_k', 'bank_v')}
    del _L1_attn_all

    def _L1_ffn_setup():
        import jax, jax.numpy as jnp
        import numpy as np
        B, T, D, E, K = (4, 512, 192, 8, 2)
        H = 4 * D
        key = jax.random.key(seed)
        k0, k1, k2, k3, k4 = jax.random.split(key, 5)
        s = 0.02
        return {'x': jax.random.normal(k0, (B, T, D), jnp.float32), 'router_w': jax.random.uniform(k1, (E, D), jnp.float32, -s * 0.1, s * 0.1), 'Wg': jax.random.uniform(k2, (E, H, D), jnp.float32, -s * 0.4, s * 0.4), 'Wu': jax.random.uniform(k3, (E, H, D), jnp.float32, -s * 0.4, s * 0.4), 'Wd': jax.random.normal(k4, (E, D, H), jnp.float32) * 0.01}
    _L1_ffn_all = _L1_ffn_setup()
    _L1_ffn_in = {k: v for k, v in _L1_ffn_all.items() if k in ('router_w', 'Wg', 'Wu', 'Wd')}
    del _L1_ffn_all
    return {'x': x, 'txt': txt, 'L0_tok_ln_gamma': _L0_tok_in['ln_gamma'], 'L0_tok_ln_beta': _L0_tok_in['ln_beta'], 'L0_tok_w': _L0_tok_in['w'], 'L0_tok_b': _L0_tok_in['b'], 'L0_attn_A_log': _L0_attn_in['A_log'], 'L0_attn_D_param': _L0_attn_in['D_param'], 'L0_attn_W_bc': _L0_attn_in['W_bc'], 'L0_attn_W_dt': _L0_attn_in['W_dt'], 'L0_attn_W_dtp': _L0_attn_in['W_dtp'], 'L0_attn_b_dt': _L0_attn_in['b_dt'], 'L0_attn_rms_scale': _L0_attn_in['rms_scale'], 'L0_ffn_W1': _L0_ffn_in['W1'], 'L0_ffn_b1': _L0_ffn_in['b1'], 'L0_ffn_W2': _L0_ffn_in['W2'], 'L0_ffn_b2': _L0_ffn_in['b2'], 'L0_ffn_Wr1': _L0_ffn_in['Wr1'], 'L0_ffn_br1': _L0_ffn_in['br1'], 'L0_ffn_Wr2': _L0_ffn_in['Wr2'], 'L0_ffn_br2': _L0_ffn_in['br2'], 'L1_attn_qkv_w': _L1_attn_in['qkv_w'], 'L1_attn_qkv_b': _L1_attn_in['qkv_b'], 'L1_attn_proj_w': _L1_attn_in['proj_w'], 'L1_attn_proj_b': _L1_attn_in['proj_b'], 'L1_attn_norm_w': _L1_attn_in['norm_w'], 'L1_attn_norm_b': _L1_attn_in['norm_b'], 'L1_attn_bank_k': _L1_attn_in['bank_k'], 'L1_attn_bank_v': _L1_attn_in['bank_v'], 'L1_ffn_router_w': _L1_ffn_in['router_w'], 'L1_ffn_Wg': _L1_ffn_in['Wg'], 'L1_ffn_Wu': _L1_ffn_in['Wu'], 'L1_ffn_Wd': _L1_ffn_in['Wd']}

def reference(x, txt, L0_tok_ln_gamma, L0_tok_ln_beta, L0_tok_w, L0_tok_b, L0_attn_A_log, L0_attn_D_param, L0_attn_W_bc, L0_attn_W_dt, L0_attn_W_dtp, L0_attn_b_dt, L0_attn_rms_scale, L0_ffn_W1, L0_ffn_b1, L0_ffn_W2, L0_ffn_b2, L0_ffn_Wr1, L0_ffn_br1, L0_ffn_Wr2, L0_ffn_br2, L1_attn_qkv_w, L1_attn_qkv_b, L1_attn_proj_w, L1_attn_proj_b, L1_attn_norm_w, L1_attn_norm_b, L1_attn_bank_k, L1_attn_bank_v, L1_ffn_router_w, L1_ffn_Wg, L1_ffn_Wu, L1_ffn_Wd):
    import jax
    import jax.numpy as jnp

    def _L0_tok_ref(x, ln_gamma, ln_beta, w, b):
        import jax, jax.numpy as jnp
        import numpy as np
        PATCH = 16
        DIM = 192
        LN_EPS = 1e-05

        def _spt_forward(x, ln_gamma, ln_beta, w, b):
            B, C, H, W = x.shape
            p = PATCH
            x_right = jnp.pad(x, ((0, 0), (0, 0), (0, 0), (1, 0)))[:, :, :, :-1]
            x_left = jnp.pad(x, ((0, 0), (0, 0), (0, 0), (0, 1)))[:, :, :, 1:]
            x_down = jnp.pad(x, ((0, 0), (0, 0), (1, 0), (0, 0)))[:, :, :-1, :]
            x_up = jnp.pad(x, ((0, 0), (0, 0), (0, 1), (0, 0)))[:, :, 1:, :]
            xc = jnp.concatenate((x, x_right, x_left, x_down, x_up), axis=1)
            C5 = 5 * C
            h, wgrid = (H // p, W // p)
            tokens = xc.reshape(B, C5, h, p, wgrid, p)
            tokens = tokens.transpose(0, 2, 4, 3, 5, 1)
            tokens = tokens.reshape(B, h * wgrid, p * p * C5)
            mean = jnp.mean(tokens, axis=-1, keepdims=True)
            var = jnp.var(tokens, axis=-1, keepdims=True)
            normed = (tokens - mean) * jax.lax.rsqrt(var + LN_EPS) * ln_gamma + ln_beta
            return jnp.einsum('bnd,de->bne', normed, w) + b
        return _spt_forward(x, ln_gamma, ln_beta, w, b)

    def _L0_attn_ref(x, A_log, D_param, W_bc, W_dt, W_dtp, b_dt, rms_scale):
        import jax, jax.numpy as jnp
        import numpy as np
        from jax import lax
        B_SZ, L, D, N, R = (1, 1024, 192, 16, 48)

        def _soft_clamp(x, lo=0.0001, hi=10.0):
            center = (hi + lo) / 2.0
            half_range = (hi - lo) / 2.0
            return center + half_range * jnp.tanh((x - center) / half_range)
        n = A_log.shape[1]
        A = -jnp.exp(A_log)
        bc = x @ W_bc
        B_sel, C_sel = (bc[..., :n], bc[..., n:])
        delta = jax.nn.softplus(x @ W_dt @ W_dtp + b_dt)
        delta = delta * lax.rsqrt(jnp.mean(delta * delta, axis=-1, keepdims=True) + 1e-06) * rms_scale
        delta = _soft_clamp(delta, 0.0001, 10.0)
        dE = delta[..., None]
        half = 0.5 * dE * A
        denom = 1.0 - half
        A_bar = (1.0 + half) / denom
        B_bar = jnp.sqrt(dE) * B_sel[:, :, None, :] / denom
        x_prev = jnp.concatenate([jnp.zeros_like(x[:, :1]), x[:, :-1]], axis=1)
        x_in = 0.5 * (x + x_prev)
        Bx = B_bar * x_in[..., None]

        def op(left, right):
            a_l, b_l = left
            a_r, b_r = right
            return (a_r * a_l, a_r * b_l + b_r)
        _, all_h = lax.associative_scan(op, (A_bar, Bx), axis=1)
        y = jnp.sum(C_sel[:, :, None, :] * all_h, axis=-1)
        return y + D_param * x

    def _L0_ffn_ref(x, W1, b1, W2, b2, Wr1, br1, Wr2, br2):
        import jax, jax.numpy as jnp
        import numpy as np
        E = 8
        K = 2
        D = 192
        F = 4 * D
        h = jax.nn.relu(jnp.einsum('bsd,hd->bsh', x, Wr1) + br1)
        score = jnp.einsum('bsd,ed->bse', h, Wr2) + br2
        _, idx = jax.lax.top_k(score, K)
        mask = (jax.nn.one_hot(idx, E) > 0).any(axis=-2)
        w = jax.nn.softmax(jnp.where(mask, score, -jnp.inf), axis=-1)
        out = jnp.zeros_like(x)
        for e in range(E):
            mid = jax.nn.relu(jnp.einsum('bsd,fd->bsf', x, W1[e]) + b1[e])
            ye = jnp.einsum('bsf,df->bsd', mid, W2[e]) + b2[e]
            out = out + w[..., e:e + 1] * ye
        return out

    def _L1_attn_ref(x, qkv_w, qkv_b, proj_w, proj_b, norm_w, norm_b, bank_k, bank_v):
        import jax, jax.numpy as jnp
        import numpy as np
        B, N, C = (16, 256, 192)
        NUM_HEADS, BANK = (12, 64)
        HEAD_DIM = C // NUM_HEADS
        LN_EPS = 1e-05

        def _split_heads_bank(bank, b):
            t = jnp.broadcast_to(bank, (b,) + bank.shape)
            return t.reshape(b, BANK, NUM_HEADS, HEAD_DIM).transpose(0, 2, 1, 3)

        def _reference_tuple_inner(x, qkv_w, qkv_b, proj_w, proj_b, norm_w, norm_b, bank_k, bank_v):
            b, n, c = x.shape
            h, d = (NUM_HEADS, HEAD_DIM)
            qkv = jnp.einsum('bnc,fc->bnf', x, qkv_w) + qkv_b
            qkv = qkv.reshape(b, n, 3, h, d).transpose(2, 0, 3, 1, 4)
            q, k, v = (qkv[0], qkv[1], qkv[2])
            k_full = jnp.concatenate([k, _split_heads_bank(bank_k, b)], axis=2)
            v_full = jnp.concatenate([v, _split_heads_bank(bank_v, b)], axis=2)
            scores = jnp.einsum('bhnd,bhmd->bhnm', q, k_full) / jnp.sqrt(jnp.asarray(d, x.dtype))
            attn = jax.nn.softmax(scores, axis=-1)
            out = jnp.einsum('bhnm,bhmd->bhnd', attn, v_full)
            out = out.transpose(0, 2, 1, 3).reshape(b, n, c)
            p = jnp.einsum('bnc,oc->bno', out, proj_w) + proj_b
            mu = jnp.mean(p, axis=-1, keepdims=True)
            var = jnp.mean(jnp.square(p - mu), axis=-1, keepdims=True)
            bank_update = (p - mu) * jax.lax.rsqrt(var + LN_EPS) * norm_w + norm_b
            return (out, bank_update)
        return _reference_tuple_inner(x, qkv_w, qkv_b, proj_w, proj_b, norm_w, norm_b, bank_k, bank_v)[0]

    def _L1_ffn_ref(x, router_w, Wg, Wu, Wd):
        import jax, jax.numpy as jnp
        import numpy as np
        B, T, D, E, K = (4, 512, 192, 8, 2)
        H = 4 * D
        Bv, Tv, Dv = x.shape
        N = Bv * Tv
        xf = x.reshape(N, Dv)
        logits = (xf @ router_w.T).astype(jnp.float32)
        top_logits, top_idx = jax.lax.top_k(logits, K)
        top_w = jax.nn.softmax(top_logits, axis=-1).astype(x.dtype)
        out = jnp.zeros_like(xf)
        for e in range(E):
            w_e = jnp.sum(top_w * (top_idx == e), axis=-1)
            h = jax.nn.silu(xf @ Wg[e].T) * (xf @ Wu[e].T)
            out = out + h @ Wd[e].T * w_e[:, None]
        return out.reshape(Bv, Tv, Dv)
    h = _L0_tok_ref(x, L0_tok_ln_gamma, L0_tok_ln_beta, L0_tok_w, L0_tok_b)
    h = jnp.concatenate([h, txt], axis=1)
    h = h + _L0_attn_ref(_layernorm(h, axis=-1), L0_attn_A_log, L0_attn_D_param, L0_attn_W_bc, L0_attn_W_dt, L0_attn_W_dtp, L0_attn_b_dt, L0_attn_rms_scale)
    h = h + _L0_ffn_ref(_layernorm(h, axis=-1), L0_ffn_W1, L0_ffn_b1, L0_ffn_W2, L0_ffn_b2, L0_ffn_Wr1, L0_ffn_br1, L0_ffn_Wr2, L0_ffn_br2)
    h = h + _L1_attn_ref(_layernorm(h, axis=-1), L1_attn_qkv_w, L1_attn_qkv_b, L1_attn_proj_w, L1_attn_proj_b, L1_attn_norm_w, L1_attn_norm_b, L1_attn_bank_k, L1_attn_bank_v)
    h = h + _L1_ffn_ref(_layernorm(h, axis=-1), L1_ffn_router_w, L1_ffn_Wg, L1_ffn_Wu, L1_ffn_Wd)
    return h

_drawn_inputs = setup_inputs


def setup_inputs(seed=0):
    import zlib

    import numpy as np

    out = dict(_drawn_inputs(seed))
    spreads = {'L0_tok_ln_gamma': (1.0, 0.2),
     'L0_tok_ln_beta': (0.0, 0.1),
     'L0_tok_b': (0.0, 0.1),
     'L0_attn_D_param': (1.0, 0.2),
     'L0_attn_rms_scale': (1.0, 0.6),
     'L1_attn_qkv_b': (0.0, 0.1),
     'L1_attn_proj_b': (0.0, 0.1),
     'L1_attn_norm_w': (1.0, 0.2),
     'L1_attn_norm_b': (0.0, 0.1)}
    factors = {'L0_ffn_b1': 8.0,
     'L0_ffn_b2': 8.0,
     'L0_ffn_br1': 7.19,
     'L0_ffn_br2': 2.737,
     'L1_attn_qkv_w': 8.0,
     'L1_attn_bank_k': 200.0,
     'L1_attn_bank_v': 200.0,
     'L1_ffn_router_w': 8.0,
     'L1_ffn_Wg': 8.0,
     'L1_ffn_Wu': 8.0,
     'L1_ffn_Wd': 8.0}
    for name, (base, spread) in spreads.items():
        noise = np.random.default_rng([zlib.crc32(name.encode()), seed]).standard_normal(out[name].shape)
        drawn = base * np.exp(spread * noise) if base else spread * noise
        out[name] = jnp.asarray(drawn.astype(out[name].dtype))
    for name, factor in factors.items():
        out[name] = (out[name] * factor).astype(out[name].dtype)
    return out
```

```python
from contextlib import ExitStack

import concourse.bass as bass
from concourse import mybir

ALU = mybir.AluOpType
ACT = mybir.ActivationFunctionType
AX = mybir.AxisListType
F32 = mybir.dt.float32
F16 = mybir.dt.float16
BF16 = mybir.dt.bfloat16
I32 = mybir.dt.int32
U32 = mybir.dt.uint32

P = 128
BATCH = 8
PATCHES = 36
TEXT = 128
SEQ = PATCHES + TEXT
D = 192
DM, DT = 128, 64
HALF = SEQ // 2
TILES = 2 * BATCH
TOKENS = BATCH * SEQ
PIECE = 2 * SEQ
LN_EPS = 1e-5
PATCH_DIM = 16 * 16 * 15
KP = PATCH_DIM // P
KCH = 5
IMG_TILES = (108, 108, 72)
STATES = 16
DT_RANK = 48
UNITS = 3
UCOLS = 4 * SEQ
E_NUM = 8
FF = 4 * D
SLOTS = 28
SLOT_ROWS = SLOTS * P
assert SLOTS == (2 * TOKENS + E_NUM * (P - 1)) // P
XROW = D + DT
W_SCALE = 64.0
LN2 = 0.6931471805599453


def chained(eng, sem, base=0):
    count = [0]

    def link(instruction):
        count[0] += 1
        instruction.then_inc(sem, 1)
        eng.wait_ge(sem, base + count[0])
    return link


def stage_semaphores(nc, ctx):
    held = []

    def give_back():
        nc.clear_and_free_semaphores(held)
        nc.all_engine_barrier()
    ctx.callback(give_back)

    def sem(name):
        held.append(nc.alloc_semaphore(name))
        return held[-1]
    return sem


def tokenizer(nc, patches, tok_w, gamma, beta, tok_b, txt, const_rows, ident, neg_half, consts, h):
    with ExitStack() as ctx:
        def sb(name, shape, dt=F32):
            return ctx.enter_context(nc.sbuf_tensor(name, shape, dt))

        def ps(name, shape, dt=F32):
            return ctx.enter_context(nc.psum_tensor(name, shape, dt))

        sem = stage_semaphores(nc, ctx)

        NCH = KP // KCH
        IMG = BATCH * PATCHES
        pt = sb("patchT", [P, KP, IMG])
        sq = sb("patch_squares", [P, 2, KCH, IMG])
        w_raw = sb("tok_w_raw", [P, KP, D])
        w_g = sb("tok_w_gamma", [P, KP, D + 1])
        w_b = sb("tok_w_beta", [P, 2, KCH, D])
        w_gs = sb("gamma_w_sum", [P, NCH, D])
        w_bs = sb("beta_w_sum", [P, NCH, D])
        g_sb = sb("gamma_sb", [P, KP])
        b_sb = sb("beta_sb", [P, KP])
        bias = sb("tok_bias", [P, D])
        ones = sb("tok_ones", [P, P])
        wsum = sb("wsum_sb", [P, D])
        bw = sb("bw_sb", [P, D])
        stat = sb("tok_stat", [P, 3, 4])
        out = sb("tok_out", [P, 3, D])
        acc = [ps(f"tok_acc{i}", [P, 512]) for i in range(3)]
        acc2 = [ps(f"tok_acc_sq{i}", [P, 512]) for i in range(3)]
        ws_ps = ps("wsum_ps", [P, 512])
        bw_ps = ps("bw_ps", [P, 512])

        vec_in = sem("vec_in")
        patch_in = [sem(f"patch_in{c}") for c in range(NCH)]
        w_in = [sem(f"w_in{c}") for c in range(NCH)]
        txt_in = sem("txt_in")
        consts_in = sem("consts_in")
        ones_set = sem("ones_set")
        ones_col = sem("ones_col")
        squared = sem("squared")
        squares_used = sem("squares_used")
        w_scaled = sem("w_scaled")
        beta_w = sem("beta_w")
        w_b_used = sem("w_b_used")
        sums_ready = sem("sums_ready")
        embedded = sem("embedded")
        dve_seq = sem("tok_dve_seq")
        var_ready = sem("var_ready")
        rstd_ready = sem("rstd_ready")
        rows_ready = sem("rows_ready")
        rows_moved = sem("rows_moved")
        block = ctx.enter_context(nc.Block())
        ks = [slice(c * KCH, (c + 1) * KCH) for c in range(NCH)]

        @block.sync
        def _(sp):
            sp.dma_start(g_sb[:], gamma.rearrange("(p k) -> p k", k=KP)).then_inc(vec_in, 16)
            sp.dma_start(b_sb[:], beta.rearrange("(p k) -> p k", k=KP)).then_inc(vec_in, 16)
            sp.dma_start(bias[:], tok_b.partition_broadcast(P)).then_inc(vec_in, 16)
            sp.dma_start(consts[:], const_rows).then_inc(consts_in, 16)
            pv = patches.rearrange("(p k) t -> p k t", k=KP)
            for c in range(NCH):
                sp.dma_start(pt[:, ks[c], :], pv[:, ks[c], :]).then_inc(patch_in[c], 16)
            row = 0
            for i, m in enumerate(IMG_TILES):
                sp.wait_ge(rows_ready, i + 1)
                for r in range(0, m, PATCHES):
                    sp.dma_start(h[0:PATCHES, 2 * row, :], out[r:r + PATCHES, i, :]).then_inc(rows_moved, 16)
                    row += 1
            sp.wait_ge(rows_moved, 16 * BATCH)
            sp.wait_ge(txt_in, 32)
            sp.wait_ge(consts_in, 16)

        @block.scalar
        def _(act):
            wv = tok_w.rearrange("(p k) n -> p k n", k=KP)
            for c in range(NCH):
                act.dma_start(w_raw[:, ks[c], :], wv[:, ks[c], :]).then_inc(w_in[c], 16)
            tv = txt.rearrange("b t d -> t b d")
            first = HALF - PATCHES
            act.dma_start(h[PATCHES:HALF, 0::2, :], tv[0:first, :, :]).then_inc(txt_in, 16)
            act.dma_start(h[0:HALF, 1::2, :], tv[first:TEXT, :, :]).then_inc(txt_in, 16)
            for c in range(NCH):
                act.wait_ge(patch_in[c], 16)
                if c >= 2:
                    act.wait_ge(squares_used, c - 1)
                nc.scalar.activation(sq[:, c % 2], pt[:, ks[c], :], ACT.Square).then_inc(squared, 1)

        @block.gpsimd
        def _(pool):
            nc.gpsimd.memset(ones[:], 1.0).then_inc(ones_set, 1)
            nc.gpsimd.memset(w_g[:, :, D:D + 1], 1.0).then_inc(ones_col, 1)
            nc.gpsimd.memset(ident[:], 0.0).then_inc(ones_set, 1)
            nc.gpsimd.memset(neg_half[:], -0.5).then_inc(ones_col, 1)
            pool.wait_ge(ones_set, 2)
            nc.gpsimd.affine_select(out=ident[:], in_=ident[:], compare_op=ALU.not_equal, fill=1.0,
                                    base=0, pattern=[[-1, P]], channel_multiplier=1).then_inc(ones_set, 1)
            pool.wait_ge(vec_in, 48)
            for c in range(NCH):
                pool.wait_ge(w_in[c], 16)
                if c >= 2:
                    pool.wait_ge(w_b_used, c - 1)
                nc.gpsimd.tensor_tensor(w_b[:, c % 2], w_raw[:, ks[c], :],
                                        b_sb[:, ks[c]].unsqueeze(2).broadcast_to([P, KCH, D]),
                                        ALU.mult).then_inc(beta_w, 1)
            for i, m in enumerate(IMG_TILES):
                pool.wait_ge(ones_col, 2)
                pool.wait_ge(var_ready, i + 1)
                nc.gpsimd.tensor_tensor(stat[0:m, i, 2:3], stat[0:m, i, 1:2], neg_half[0:m, 0:1],
                                        ALU.pow).then_inc(rstd_ready, 1)

        @block.vector
        def _(dve):
            link = chained(dve, dve_seq)
            dve.wait_ge(vec_in, 48)
            dve.wait_ge(ones_col, 1)
            for c in range(NCH):
                dve.wait_ge(w_in[c], 16)
                nc.vector.tensor_tensor(w_g[:, ks[c], 0:D], w_raw[:, ks[c], :],
                                        g_sb[:, ks[c]].unsqueeze(2).broadcast_to([P, KCH, D]),
                                        ALU.mult).then_inc(w_scaled, 1)
                dve.wait_ge(beta_w, c + 1)
                nc.vector.tensor_reduce(w_bs[:, c, :], w_b[:, c % 2].rearrange("p k n -> p n k"),
                                        AX.X, ALU.add).then_inc(w_b_used, 1)
                dve.wait_ge(w_scaled, c + 1)
                nc.vector.tensor_reduce(w_gs[:, c, :], w_g[:, ks[c], 0:D].rearrange("p k n -> p n k"),
                                        AX.X, ALU.add).then_inc(sums_ready, 1)
            dve.wait_ge(embedded, 1)
            link(nc.vector.tensor_copy(wsum[:], ws_ps[:, 0:D]))
            link(nc.vector.tensor_tensor(bw[:], bw_ps[:, 0:D], bias[:], ALU.add))
            for i, m in enumerate(IMG_TILES):
                s = stat[0:m, i, :]
                link(nc.vector.tensor_scalar(s[:, 0:1], acc[i][0:m, D:D + 1], -1.0 / PATCH_DIM, None, ALU.mult))
                link(nc.vector.tensor_tensor(s[:, 3:4], s[:, 0:1], s[:, 0:1], ALU.mult))
                link(nc.vector.scalar_tensor_tensor(out=s[:, 1:2], in0=acc2[i][0:m, 0:1], scalar=1.0 / PATCH_DIM,
                                                    in1=s[:, 3:4], op0=ALU.mult, op1=ALU.subtract))
                nc.vector.tensor_scalar(s[:, 1:2], s[:, 1:2], LN_EPS, None, ALU.add).then_inc(var_ready, 1)
                link(nc.vector.scalar_tensor_tensor(out=out[0:m, i, :], in0=wsum[0:m, :], scalar=s[:, 0:1],
                                                    in1=acc[i][0:m, 0:D], op0=ALU.mult, op1=ALU.add))
                dve.wait_ge(rstd_ready, i + 1)
                nc.vector.scalar_tensor_tensor(out=out[0:m, i, :], in0=out[0:m, i, :], scalar=s[:, 2:3],
                                               in1=bw[0:m, :], op0=ALU.mult,
                                               op1=ALU.add).then_inc(rows_ready, 1)

        @block.tensor
        def _(pe):
            pe.wait_ge(ones_set, 3)
            for c in range(NCH):
                pe.wait_ge(patch_in[c], 16)
                pe.wait_ge(w_scaled, c + 1)
                for k in range(c * KCH, (c + 1) * KCH):
                    col = 0
                    for i, m in enumerate(IMG_TILES):
                        last = nc.tensor.matmul(acc[i][0:m, 0:D + 1], pt[:, k, col:col + m], w_g[:, k, :],
                                                start=k == 0, stop=k == KP - 1)
                        col += m
                pe.wait_ge(squared, c + 1)
                for k in range(KCH):
                    col = 0
                    for i, m in enumerate(IMG_TILES):
                        last = nc.tensor.matmul(acc2[i][0:m, 0:1], sq[:, c % 2, k, col:col + m], ones[:, 0:1],
                                                start=c + k == 0, stop=c == NCH - 1 and k == KCH - 1)
                        col += m
                last.then_inc(squares_used, 1)
                pe.wait_ge(sums_ready, c + 1)
                pe.wait_ge(w_b_used, c + 1)
                nc.tensor.matmul(ws_ps[:, 0:D], ones[:], w_gs[:, c, :], start=c == 0, stop=c == NCH - 1)
                last = nc.tensor.matmul(bw_ps[:, 0:D], ones[:], w_bs[:, c, :], start=c == 0, stop=c == NCH - 1)
            last.then_inc(embedded, 1)


def normalize(nc, name, h, xn, ident, neg_half, x_main, x_tail, split_tail, row_store=None):
    with ExitStack() as ctx:
        stage_sem = stage_semaphores(nc, ctx)

        def sem(s):
            return stage_sem(f"{name}_{s}")

        st = ctx.enter_context(nc.sbuf_tensor(f"{name}_stats", [HALF, TILES, 6], F32))
        mv = ctx.enter_context(nc.sbuf_tensor(f"{name}_mv", [HALF, TILES, 2], F32))
        rstd = ctx.enter_context(nc.sbuf_tensor(f"{name}_rstd", [HALF, TILES], F32))
        tp = ctx.enter_context(nc.psum_tensor(f"{name}_tp", [P, BATCH, 512], F32))
        stats = sem("stats")
        moments = sem("moments")
        rstd_ready = sem("rstd_ready")
        normed = sem("normed")
        turned = sem("turned")
        stored = sem("stored")
        block = ctx.enter_context(nc.Block())

        @block.vector
        def _(dve):
            for t in range(TILES):
                nc.vector.bn_stats(st[:, t, :], h[:, t, :]).then_inc(stats, 1)
            for t in range(TILES):
                dve.wait_ge(stats, t + 1)
                nc.vector.bn_aggr(mv[:, t, :], st[:, t, :]).then_inc(moments, 1)
            dve.wait_ge(moments, TILES)
            nc.vector.tensor_scalar(rstd[:], mv[:, :, 1], LN_EPS, None, ALU.add).then_inc(moments, 1)
            dve.wait_ge(rstd_ready, 1)
            for t in range(TILES):
                nc.vector.tensor_scalar(xn[:, t, 0:D], h[:, t, :], mv[:, t, 0:1], rstd[:, t:t + 1],
                                        ALU.subtract, ALU.mult).then_inc(normed, 1)
            if row_store is not None:
                dve.wait_ge(normed, TILES)
                nc.vector.tensor_copy(xn[:, :, D:XROW], xn[:, :, DM:D]).then_inc(normed, 1)

        @block.gpsimd
        def _(pool):
            pool.wait_ge(moments, TILES + 1)
            nc.gpsimd.tensor_tensor(rstd[:], rstd[:], neg_half[0:HALF, 0:TILES], ALU.pow).then_inc(rstd_ready, 1)

        @block.sync
        def _(sp):
            if row_store is not None:
                sp.wait_ge(normed, TILES + 1)
                sp.dma_start(row_store.rearrange("(t p) c -> p t c", p=HALF), xn[:]).then_inc(stored, 16)
                sp.wait_ge(stored, 16)

        @block.tensor
        def _(pe):
            for b in range(BATCH):
                upper = split_tail and b >= BATCH // 2
                for t in (2 * b, 2 * b + 1):
                    pe.wait_ge(normed, t + 1)
                    c = t % 2 * HALF
                    nc.tensor.transpose(tp[:, b, c:c + HALF], xn[:, t, 0:DM], ident[0:HALF, 0:HALF])
                    c += SEQ
                    if upper:
                        last = nc.tensor.transpose(tp[:, b, c:c + HALF], xn[:, t, D - P:D], ident[0:HALF, 0:HALF])
                    else:
                        last = nc.tensor.transpose(tp[0:DT, b, c:c + HALF], xn[:, t, DM:D], ident[0:HALF, 0:HALF])
                last.then_inc(turned, 1)

        @block.scalar
        def _(act):
            for b in range(BATCH):
                upper = split_tail and b >= BATCH // 2
                rows = slice(DT, P) if upper else slice(0, DT)
                col = (b - BATCH // 2 if upper else b) * SEQ
                act.wait_ge(turned, b + 1)
                nc.scalar.activation(x_main[:, b * SEQ:(b + 1) * SEQ], tp[:, b, 0:SEQ], ACT.Copy)
                nc.scalar.activation(x_tail[rows, col:col + SEQ], tp[rows, b, SEQ:2 * SEQ], ACT.Copy)


def state_scan(nc, h, xd, ident, w_bc, w_dt, w_dtp, dt_vecs, a_log):
    ALL = UNITS * UCOLS
    MAINC = 2 * UCOLS
    CLAMP_LO, CLAMP_HI = 1e-4, 10.0
    CENTER, REACH = (CLAMP_HI + CLAMP_LO) / 2, (CLAMP_HI - CLAMP_LO) / 2
    NBC = 2 * STATES
    with ExitStack() as ctx:
        def sb(name, shape, dt=F32):
            return ctx.enter_context(nc.sbuf_tensor(name, shape, dt))

        sem = stage_semaphores(nc, ctx)

        bc3_m = sb("w_bc3_main", [P, 3 * NBC])
        bc3_t = sb("w_bc3_tail", [P, 3 * NBC])
        dt_m = sb("w_dt_main", [P, DT_RANK])
        dt_t = sb("w_dt_tail", [P, DT_RANK])
        dtp = sb("w_dtp", [DT_RANK, D])
        vecs = sb("dt_vecs", [P, 2, 3])
        al = sb("a_log_sb", [P, 2, STATES])
        a_tanh = sb("a_tanh_bias", [P, 2, STATES])
        a_sig = sb("a_sigmoid_bias", [P, 2, STATES])
        clamp_b = sb("clamp_bias", [P, 1])
        clamp_eps = sb("rms_eps", [P, 1])
        center_b = sb("clamp_center", [P, 1])
        ones = sb("scan_ones", [P, P])
        sel = sb("selector", [3 * NBC, NBC, 2 * P], BF16)
        no_state = sb("no_state", [P, 4])
        zeros = sb("scan_zeros", [3 * NBC, P], BF16)
        parts = sb("bc_parts", [3 * NBC, MAINC], BF16)
        low = sb("bc_low", [3 * NBC, MAINC], BF16)
        rest = sb("bc_rest", [3 * NBC, MAINC])
        dtT = sb("dtT", [DT_RANK, MAINC])
        t1 = sb("delta_abs", [P, ALL])
        t2 = sb("delta_tmp", [P, ALL])
        ln_d = sb("ln_delta", [P, ALL])
        G = sb("input_gain", [P, ALL])
        rms = sb("delta_rms", [P, MAINC])
        yd = sb("scan_out", [P, ALL])
        A = sb("decay", [P, 2, UCOLS])
        R = sb("gate", [P, 2, UCOLS])
        W = sb("gated_input", [P, 2, UCOLS])
        BX = sb("driven", [P, 2, UCOLS])
        H = sb("state", [P, 2, UCOLS])
        CH = sb("read_state", [P, 2, UCOLS])

        loaded = sem("scan_loaded")
        consts = sem("scan_consts")
        selected = sem("sel_ready")
        bias_ready = sem("a_bias_ready")
        bc_done = sem("bc_done")
        parts_seq = sem("parts_seq")
        dt_done = sem("dt_done")
        dt_kept = sem("dt_kept")
        delta_done = sem("delta_done")
        act_seq = sem("scan_act_seq")
        rms_summed = sem("rms_summed")
        squares = sem("delta_squares")
        softplus = sem("softplus_ready")
        scaled = sem("delta_scaled")
        gain = sem("gain_ready")
        pre_dve = sem("scan_pre_dve")

        with ExitStack() as pctx:
            pbc = pctx.enter_context(nc.psum_tensor("bc_ps", [P, 4, 512], F32))
            pdt = pctx.enter_context(nc.psum_tensor("dt_ps", [P, 4, 512], F32))
            block = pctx.enter_context(nc.Block())
            x_rows = [(slice(0, DT), g * PIECE) if g < 2 else (slice(DT, P), (g - 2) * PIECE) for g in range(4)]

            @block.sync
            def _(sp):
                for half in (slice(0, DT), slice(DT, P)):
                    sp.dma_start(bc3_t[half, :].rearrange("p (a n) -> p a n", a=3),
                                 w_bc[DM:D, :].unsqueeze(1).broadcast_to([DT, 3, NBC])).then_inc(loaded, 16)
                    sp.dma_start(dt_t[half, :], w_dt[DM:D, :]).then_inc(loaded, 16)
                    for i, v in enumerate(dt_vecs):
                        sp.dma_start(vecs[half, 1, i:i + 1], v[DM:D].unsqueeze(1)).then_inc(loaded, 16)
                    sp.dma_start(al[half, 1, :], a_log[DM:D, :]).then_inc(loaded, 16)
                sp.dma_start(bc3_m[:].rearrange("p (a n) -> p a n", a=3),
                             w_bc[0:DM, :].unsqueeze(1).broadcast_to([DM, 3, NBC])).then_inc(loaded, 16)
                sp.dma_start(dt_m[:], w_dt[0:DM, :]).then_inc(loaded, 16)
                sp.dma_start(dtp[:], w_dtp).then_inc(loaded, 16)
                for i, v in enumerate(dt_vecs):
                    sp.dma_start(vecs[:, 0, i:i + 1], v[0:DM].unsqueeze(1)).then_inc(loaded, 16)
                sp.dma_start(al[:, 0, :], a_log[0:DM, :]).then_inc(loaded, 16)
            LOADS = 16 * (2 * 6 + 7)

            @block.gpsimd
            def _(pool):
                nc.gpsimd.memset(ones[:], 1.0).then_inc(consts, 1)
                nc.gpsimd.memset(clamp_b[:], -CENTER / REACH).then_inc(consts, 1)
                nc.gpsimd.memset(no_state[:], 0.0).then_inc(consts, 1)
                nc.gpsimd.memset(zeros[:], 0.0).then_inc(consts, 1)
                nc.gpsimd.memset(sel[:], 0.0).then_inc(selected, 1)
                pool.wait_ge(selected, 1)
                mid = sel[:, :, DT:DT + P]
                for a in range(3):
                    nc.gpsimd.affine_select(out=mid, in_=mid, compare_op=ALU.not_equal, fill=1.0,
                                            base=-a * NBC, pattern=[[-1, NBC], [0, P]],
                                            channel_multiplier=1).then_inc(selected, 1)
                    pool.wait_ge(selected, 2 + a)

            @block.tensor
            def _(pe):
                pe.wait_ge(loaded, LOADS)
                pe.wait_ge(consts, 2)
                for g, (rows, c) in enumerate(x_rows):
                    o = pbc[0:3 * NBC, g, 0:PIECE]
                    nc.tensor.matmul(o, bc3_m[:], xd[:, g * PIECE:(g + 1) * PIECE], start=True, stop=False)
                    last = nc.tensor.matmul(o, bc3_t[rows, :], xd[rows, MAINC + c:MAINC + c + PIECE],
                                            start=False, stop=True)
                last.then_inc(bc_done, 1)
                for g, (rows, c) in enumerate(x_rows):
                    o = pdt[0:DT_RANK, g, 0:PIECE]
                    nc.tensor.matmul(o, dt_m[:], xd[:, g * PIECE:(g + 1) * PIECE], start=True, stop=False)
                    last = nc.tensor.matmul(o, dt_t[rows, :], xd[rows, MAINC + c:MAINC + c + PIECE],
                                            start=False, stop=True)
                last.then_inc(dt_done, 1)
                pe.wait_ge(dt_kept, 1)
                for g in range(4):
                    last = nc.tensor.matmul(pdt[:, g, 0:PIECE], dtp[:, 0:DM], dtT[:, g * PIECE:(g + 1) * PIECE],
                                            start=True, stop=True)
                last.then_inc(delta_done, 1)
                pe.wait_ge(parts_seq, 2)
                for g, (rows, c) in enumerate(x_rows):
                    last = nc.tensor.matmul(pbc[rows, g % 2, 0:PIECE], dtp[:, DM:D], dtT[:, g * PIECE:(g + 1) * PIECE],
                                            start=True, stop=True, skip_group_check=True)
                last.then_inc(delta_done, 1)
                pe.wait_ge(squares, 1)
                for g, (rows, c) in enumerate(x_rows):
                    o = pdt[:, g, 0:PIECE]
                    nc.tensor.matmul(o, ones[:], t2[:, g * PIECE:(g + 1) * PIECE], start=True, stop=False)
                    last = nc.tensor.matmul(o, ones[rows, :], t2[rows, MAINC + c:MAINC + c + PIECE],
                                            start=False, stop=True)
                last.then_inc(rms_summed, 1)

            @block.scalar
            def _(act):
                link = chained(act, act_seq)
                act.wait_ge(dt_done, 1)
                nc.scalar.activation(dtT[:].rearrange("p (g c) -> p g c", g=4), pdt[0:DT_RANK, :, 0:PIECE],
                                     ACT.Copy).then_inc(dt_kept, 1)
                spans = ((0, pdt[:, :, 0:PIECE], slice(0, MAINC), 4, 0),
                         (1, pbc[:, 0:2, 0:PIECE], slice(MAINC, ALL), 2, 1))
                act.wait_ge(loaded, LOADS)
                for i, src, cols, n, w in spans:
                    act.wait_ge(delta_done, i + 1)
                    nc.scalar.activation(t1[:, cols].rearrange("p (g c) -> p g c", g=n), src, ACT.Abs,
                                         bias=vecs[:, w, 0:1]).then_inc(act_seq, 1)
                    nc.scalar.activation(ln_d[:, cols].rearrange("p (g c) -> p g c", g=n), src, ACT.Relu,
                                         bias=vecs[:, w, 0:1]).then_inc(act_seq, 1)
                act.wait_ge(act_seq, 4)
                link = chained(act, act_seq, 4)
                link(nc.scalar.activation(t1[:], t1[:], ACT.Exp, scale=-1.0))
                nc.scalar.activation(t1[:], t1[:], ACT.Ln, bias=1.0).then_inc(softplus, 1)
                act.wait_ge(rms_summed, 1)
                act.wait_ge(pre_dve, 1)
                link(nc.scalar.activation(rms[:].rearrange("p (g c) -> p g c", g=4), pdt[:, :, 0:PIECE], ACT.Ln,
                                          scale=1.0 / D, bias=clamp_eps[:, 0:1]))
                link(nc.scalar.activation(rms[:], rms[:], ACT.Exp, scale=-0.5))
                act.wait_ge(scaled, 1)
                act.wait_ge(consts, 2)
                link(nc.scalar.activation(t1[:], t1[:], ACT.Tanh, scale=1.0 / REACH, bias=clamp_b[:, 0:1]))
                link(nc.scalar.activation(ln_d[:], t1[:], ACT.Ln, scale=REACH, bias=center_b[:, 0:1]))
                nc.scalar.activation(t2[:], ln_d[:], ACT.Exp, scale=0.5).then_inc(gain, 1)

            @block.vector
            def _(dve):
                link = chained(dve, parts_seq)
                dve.wait_ge(bc_done, 1)
                v = pbc[0:3 * NBC, :, 0:PIECE]
                as4 = lambda t: t.rearrange("p (g c) -> p g c", g=4)
                link(nc.vector.tensor_copy(as4(parts[:]), v))
                link(nc.vector.tensor_tensor(as4(rest[:]), v, as4(parts[:]), ALU.subtract))
                link(nc.vector.tensor_copy(low[:], rest[:]))
                nc.vector.tensor_copy(parts[NBC:2 * NBC, :], low[NBC:2 * NBC, :]).then_inc(parts_seq, 1)
                link(nc.vector.tensor_tensor(rest[:], rest[:], low[:], ALU.subtract))
                dve.wait_ge(parts_seq, 5)
                nc.vector.tensor_copy(parts[2 * NBC:3 * NBC, :], rest[2 * NBC:3 * NBC, :]).then_inc(parts_seq, 1)

                pre = chained(dve, pre_dve)
                nc.vector.memset(center_b[:], CENTER)
                pre(nc.vector.memset(clamp_eps[:], 1e-6))
                dve.wait_ge(loaded, LOADS)
                nc.vector.tensor_scalar(a_tanh[:], al[:], -LN2, -0.5, ALU.add, ALU.mult).then_inc(bias_ready, 1)
                nc.vector.tensor_scalar(a_sig[:], al[:], -LN2, -1.0, ALU.add, ALU.mult).then_inc(bias_ready, 1)
                rows = lambda t: t.rearrange("p (r c) -> p r c", c=SEQ)
                nc.vector.tensor_tensor(rows(G[:])[:, :, 1:SEQ], rows(xd[:])[:, :, 1:SEQ],
                                        rows(xd[:])[:, :, 0:SEQ - 1], ALU.add).then_inc(pre_dve, 1)
                pre(nc.vector.tensor_copy(rows(G[:])[:, :, 0:1], rows(xd[:])[:, :, 0:1]))
                dve.wait_ge(pre_dve, 3)
                dve.wait_ge(softplus, 1)
                dve.wait_ge(act_seq, 5)
                pre = chained(dve, pre_dve, 3)
                pre(nc.vector.tensor_tensor(t1[:], t1[:], ln_d[:], ALU.add))
                nc.vector.tensor_tensor(t2[:], t1[:], t1[:], ALU.mult).then_inc(squares, 1)
                dve.wait_ge(act_seq, 7)
                nc.vector.scalar_tensor_tensor(out=t1[:, 0:MAINC], in0=t1[:, 0:MAINC], scalar=vecs[:, 0, 1:2],
                                               in1=rms[:], op0=ALU.mult, op1=ALU.mult).then_inc(pre_dve, 1)
                for half, c in ((slice(0, DT), 0), (slice(DT, P), UCOLS)):
                    nc.vector.scalar_tensor_tensor(out=t1[half, MAINC:ALL], in0=t1[half, MAINC:ALL],
                                                   scalar=vecs[half, 1, 1:2], in1=rms[half, c:c + UCOLS],
                                                   op0=ALU.mult, op1=ALU.mult).then_inc(pre_dve, 1)
                dve.wait_ge(pre_dve, 7)
                nc.vector.memset(H[:, 0, 0:1], 0.0).then_inc(scaled, 1)
                dve.wait_ge(gain, 1)
                pre = chained(dve, pre_dve, 7)
                pre(nc.vector.scalar_tensor_tensor(out=G[:], in0=G[:], scalar=0.5, in1=t2[:],
                                                   op0=ALU.mult, op1=ALU.mult))

        decay = sem("decay_ready")
        gate = sem("gate_ready")
        reset = sem("reset_done")
        gated = sem("gated_ready")
        b_ready = sem("b_spread")
        c_ready = sem("c_spread")
        driven = sem("driven_ready")
        state = sem("state_ready")
        read = sem("read_ready")
        summed = sem("state_summed")
        y_kept = sem("y_kept")
        with ExitStack() as pctx:
            pb = pctx.enter_context(nc.psum_tensor("b_ps", [P, 2, 512], F32))
            pc = pctx.enter_context(nc.psum_tensor("c_ps", [P, 2, 512], F32))
            py = pctx.enter_context(nc.psum_tensor("y_ps", [P, 2, 512], F32))
            block = pctx.enter_context(nc.Block())
            two = lambda t: t.rearrange("p (g c) -> p g c", g=2)

            def all_steps(eng, step):
                for u in range(UNITS):
                    if u == 0:
                        for j in range(4):
                            step(u, 0, j)
                    with eng.Fori(1 if u == 0 else 0, STATES // 4 - 1) as k:
                        for j in range(4):
                            step(u, k, j)
                    for j in range(4):
                        step(u, STATES // 4 - 1, j)

            def number(u, k, j):
                return u * STATES + 4 * k + j

            def is_start(u, k):
                return u == 0 and isinstance(k, int) and k == 0

            def unit_cols(u):
                return slice(u * UCOLS, (u + 1) * UCOLS)

            @block.scalar
            def _(act):
                def step(u, k, j):
                    i, s, w = number(u, k, j), j % 2, u // 2
                    if not is_start(u, k) or j >= 2:
                        act.wait_ge(state, i - 1)
                        act.wait_ge(gated, i - 1)
                    nc.scalar.activation(A[:, s], ln_d[:, unit_cols(u)], ACT.Tanh, scale=-0.5,
                                         bias=a_tanh[:, w, bass.ds(4 * k + j, 1)]).then_inc(decay, 1)
                    nc.scalar.activation(R[:, s], ln_d[:, unit_cols(u)], ACT.Sigmoid, scale=-1.0,
                                         bias=a_sig[:, w, bass.ds(4 * k + j, 1)]).then_inc(gate, 1)
                act.wait_ge(bias_ready, 2)
                all_steps(act, step)

            @block.gpsimd
            def _(pool):
                def step(u, k, j):
                    i, s = number(u, k, j), j % 2
                    pool.wait_ge(decay, i + 1)
                    nc.gpsimd.tensor_tensor(A[:, s].rearrange("p (r c) -> p r c", c=SEQ)[:, :, 0],
                                            no_state[:], no_state[:], ALU.mult).then_inc(reset, 1)
                    pool.wait_ge(gate, i + 1)
                    if not is_start(u, k) or j >= 2:
                        pool.wait_ge(driven, i - 1)
                    nc.gpsimd.tensor_tensor(W[:, s], R[:, s], G[:, unit_cols(u)], ALU.mult).then_inc(gated, 1)
                pool.wait_ge(consts, 4)
                all_steps(pool, step)

            @block.vector
            def _(dve):
                def drive(i, s, start=False):
                    dve.wait_ge(gated, i + 1)
                    dve.wait_ge(b_ready, i + 1)
                    nc.vector.tensor_tensor(two(BX[:, s]), two(W[:, s]), pb[:, :, 0:PIECE],
                                            ALU.mult).then_inc(driven, 1)

                def step(u, k, j):
                    i, s = number(u, k, j), j % 2
                    end = isinstance(k, int) and k == STATES // 4 - 1 and j == 3
                    dve.wait_ge(reset, i + 1)
                    dve.wait_ge(driven, i + 1)
                    if not is_start(u, k) or j >= 2:
                        dve.wait_ge(read, i - 1)
                    nc.vector.tensor_tensor_scan(H[:, s], A[:, s], BX[:, s], 0.0, ALU.mult,
                                                 ALU.add).then_inc(state, 1)
                    if not (end and u == UNITS - 1):
                        drive(i + 1, 1 - s)
                    dve.wait_ge(state, i + 1)
                    dve.wait_ge(c_ready, i + 1)
                    if not is_start(u, k) or j >= 2:
                        dve.wait_ge(summed, i - 1)
                    nc.vector.tensor_tensor(two(CH[:, s]), two(H[:, s]), pc[:, :, 0:PIECE],
                                            ALU.mult).then_inc(read, 1)
                    if end:
                        dve.wait_ge(summed, i + 1)
                        nc.vector.scalar_tensor_tensor(
                            out=two(yd[:, unit_cols(u)]), in0=two(xd[:, unit_cols(u)]),
                            scalar=vecs[:, u // 2, 2:3], in1=py[:, :, 0:PIECE], op0=ALU.mult,
                            op1=ALU.add).then_inc(y_kept, 1)
                drive(0, 0)
                all_steps(dve, step)

            @block.tensor
            def _(pe):
                def spread(o, u, row, done):
                    for g in range(2):
                        if u < 2:
                            c = (2 * u + g) * PIECE
                            last = nc.tensor.matmul(o[:, g, 0:PIECE], window(row, DT), parts[:, c:c + PIECE],
                                                    start=True, stop=True)
                        else:
                            for side in range(2):
                                c = (2 * side + g) * PIECE
                                last = nc.tensor.matmul(o[:, g, 0:PIECE], window(row, P * (1 - side)),
                                                        parts[:, c:c + PIECE], start=side == 0, stop=side == 1)
                    last.then_inc(done, 1)

                def window(row, at):
                    return sel[:, bass.ds(row, 1), at:at + P].rearrange("p a m -> p (a m)")

                def step(u, k, j):
                    i, s = number(u, k, j), j % 2
                    final = isinstance(k, int) and k == STATES // 4 - 1
                    if not (final and j >= 2):
                        pe.wait_ge(driven, i + 2)
                        spread(pb, u, 4 * k + j + 2, b_ready)
                    elif u < UNITS - 1:
                        pe.wait_ge(driven, i + 2)
                        spread(pb, u + 1, j - 2, b_ready)
                    pe.wait_ge(read, i + 1)
                    if not (final and j == 3):
                        spread(pc, u, STATES + 4 * k + j + 1, c_ready)
                    elif u < UNITS - 1:
                        spread(pc, u + 1, STATES, c_ready)
                    for g in range(2):
                        last = nc.tensor.matmul(py[:, g, 0:PIECE], ident[:], CH[:, s, g * PIECE:(g + 1) * PIECE],
                                                start=False, stop=final and j == 3)
                    last.then_inc(summed, 1)
                    if final and j == 3 and u < UNITS - 1:
                        pe.wait_ge(y_kept, u + 1)
                        open_sum()

                def open_sum():
                    for g in range(2):
                        nc.tensor.matmul(py[:, g, 0:PIECE], zeros[:], parts[:, 0:PIECE], start=True, stop=False)
                pe.wait_ge(parts_seq, 6)
                pe.wait_ge(selected, 4)
                pe.wait_ge(consts, 4)
                open_sum()
                spread(pb, 0, 0, b_ready)
                spread(pc, 0, STATES, c_ready)
                pe.wait_ge(driven, 1)
                spread(pb, 0, 1, b_ready)
                all_steps(pe, step)

        turned = sem("scan_turned")
        added = sem("scan_added")
        with ExitStack() as pctx:
            tp = pctx.enter_context(nc.psum_tensor("scan_tp", [P, 8, 512], F32))
            block = pctx.enter_context(nc.Block())

            @block.tensor
            def _(pe):
                for t in range(TILES):
                    if t >= 8:
                        pe.wait_ge(added, t - 7)
                    rows = slice(0, DT) if t < TILES // 2 else slice(DT, P)
                    c = t * HALF
                    tail = MAINC + (t % (TILES // 2)) * HALF
                    nc.tensor.transpose(tp[0:HALF, t % 8, 0:DM], yd[:, c:c + HALF], ident[:])
                    nc.tensor.transpose(tp[0:HALF, t % 8, DM:D], yd[rows, tail:tail + HALF],
                                        ident[rows, rows]).then_inc(turned, 1)

            @block.vector
            def _(dve):
                for t in range(TILES):
                    dve.wait_ge(turned, t + 1)
                    nc.vector.tensor_tensor(h[:, t, :], h[:, t, :], tp[0:HALF, t % 8, 0:D], ALU.add).then_inc(added, 1)


CONSTS = {"upper": HALF, "count": P, "rank": E_NUM, "within": E_NUM * TILES, "steps": 11, "tile": TILES, "row": 1}


def const_table():
    import numpy as np
    p = np.arange(P)[:, None]
    parts = [
        p < np.arange(HALF),
        np.broadcast_to(np.arange(P), (P, P)),
        np.broadcast_to(E_NUM - np.arange(E_NUM), (P, E_NUM)),
        np.broadcast_to(np.arange(E_NUM * TILES) % TILES > 0, (P, E_NUM * TILES)),
        np.broadcast_to(np.arange(11) * P, (P, 11)),
        np.broadcast_to(np.arange(TILES), (P, TILES)),
        np.broadcast_to(p, (P, 1)),
    ]
    return np.concatenate([np.asarray(x, np.float32) for x in parts], axis=1)


def split_weights(nc, name, packed, wt, n_up):
    up = n_up * FF
    down = FF // P * D
    with ExitStack() as ctx:
        stage_sem = stage_semaphores(nc, ctx)

        def sem(s):
            return stage_sem(f"{name}_{s}")

        raw = ctx.enter_context(nc.sbuf_tensor(f"{name}_raw", [P, 2, 2 * up + down], F32))
        arrived = [sem("arrived0"), sem("arrived1")]
        high = sem("high")
        low = sem("low")
        block = ctx.enter_context(nc.Block())

        def pair(e):
            d = wt[:, e, 3 * up:].rearrange("p (c s n) -> p c s n", s=2, n=D)
            return d[:, :, 0, :], d[:, :, 1, :]

        def raw_down(e):
            return raw[:, e % 2, 2 * up:].rearrange("p (c n) -> p c n", n=D)

        @block.sync
        def _(sp):
            for e in range(E_NUM):
                if e >= 2:
                    sp.wait_ge(low, e - 1)
                sp.dma_start(raw[:, e % 2, :], packed[e]).then_inc(arrived[e % 2], 16)

        @block.scalar
        def _(act):
            for e in range(E_NUM):
                act.wait_ge(arrived[e % 2], 16 * (e // 2 + 1))
                nc.scalar.activation(wt[:, e, 0:2 * up], raw[:, e % 2, 0:2 * up], ACT.Copy, scale=W_SCALE)
                nc.scalar.activation(pair(e)[0], raw_down(e), ACT.Copy, scale=W_SCALE).then_inc(high, 1)

        @block.vector
        def _(dve):
            for e in range(E_NUM):
                r = raw[:, e % 2]
                dve.wait_ge(high, e + 1)
                for out, full, hi in (
                    (wt[:, e, 2 * up:3 * up], r[:, 0:up], wt[:, e, 0:up]),
                    (wt[DT:P, e, up:2 * up], r[DT:P, up:2 * up], wt[DT:P, e, up:2 * up]),
                    (pair(e)[1], raw_down(e), pair(e)[0]),
                ):
                    last = nc.vector.scalar_tensor_tensor(out=out, in0=full, scalar=W_SCALE, in1=hi,
                                                          op0=ALU.mult, op1=ALU.subtract)
                last.then_inc(low, 1)


def route(nc, name, x_main, x_tail, consts, hidden, router, router_bias, gate_w, pair_slot, slot_token, slot_expert):
    with ExitStack() as ctx:
        def sb(s, shape, dt=F32):
            return ctx.enter_context(nc.sbuf_tensor(f"{name}_{s}", shape, dt))

        def ps(s, shape):
            return ctx.enter_context(nc.psum_tensor(f"{name}_{s}", shape, F32))

        stage_sem = stage_semaphores(nc, ctx)

        def sem(s):
            return stage_sem(f"{name}_{s}")

        TE = [HALF, TILES, E_NUM]
        rw_m = sb("rw_main", [P, E_NUM])
        rw_t = sb("rw_tail", [DT, E_NUM])
        r_bias = sb("r_bias", [HALF, E_NUM])
        if hidden is not None:
            w1_m = sb("w1_main", [P, D])
            w1_t = sb("w1_tail", [DT, D])
            b1_m = sb("b1_main", [P, 1])
            b1_t = sb("b1_tail", [DT, 1])
            h_main = sb("h_main", [P, TOKENS])
            h_tail = sb("h_tail", [DT, TOKENS])
        upper = sb("upper", [HALF, HALF], BF16)
        ones = sb("ones", [HALF, P], BF16)
        score = sb("score", TE)
        score2 = sb("score2", TE)
        key = sb("key", TE)
        first = sb("first", TE)
        second = sb("second", TE)
        both = sb("both", TE, BF16)
        best = sb("best", [HALF, 4, TILES])
        totals = sb("totals", [P, E_NUM, TILES])
        running = sb("running", [P, E_NUM, TILES])
        over = sb("over", [P, E_NUM, 11])
        e_tiles = sb("e_tiles", [P, E_NUM])
        e_end = sb("e_end", [P, E_NUM])
        e_start = sb("e_start", [P, E_NUM])
        e_ones = sb("e_ones", [P, E_NUM])
        pos = sb("pos", TE)
        slot_f = sb("slot_f", [HALF, 2, TILES])
        slot_hi = sb("slot_hi", [HALF, 2, TILES], I32)
        slot_lo = sb("slot_lo", [HALF, 2, TILES], I32)
        hi_f = sb("hi_f", [HALF, 2 * TILES])
        lo_f = sb("lo_f", [HALF, 2 * TILES])
        passed = sb("passed", [P, SLOTS, E_NUM])
        passed_n = sb("passed_n", [P, SLOTS])
        in_tile = sb("in_tile", [HALF, 2 * TILES, SLOTS])
        ids = sb("ids", [HALF, 2 * TILES, 2, SLOTS], BF16)
        in_row = sb("in_row", [HALF, 2 * TILES, P], BF16)
        token_hi = sb("token_hi", [P, SLOTS])
        token_f = sb("token_f", [P, SLOTS])
        hp = ps("hidden_ps", [P, 2, 2, 512]) if hidden is not None else None
        sp_ = ps("score_ps", [P, 512])
        cp = ps("before_ps", [P, 512])
        tp = ps("totals_ps", [P, 512])
        ip = ps("ids_ps", [P, 512])

        loaded = sem("loaded")
        hid_done = sem("hid_done")
        hid_kept = sem("hid_kept")
        scored = sem("scored")
        seq = sem("dve_seq")
        margin = sem("margin")
        raised = sem("raised")
        counted = sem("counted")
        chosen = sem("chosen")
        spread = sem("spread")
        inverted = sem("inverted")
        block = ctx.enter_context(nc.Block())

        at, view = 0, {}
        for n, width in CONSTS.items():
            view[n] = consts[:, at:at + width]
            at += width
        loads = [(rw_m[:], router[0:DM, :]), (rw_t[:], router[DM:D, :])]
        if router_bias is not None:
            loads.append((r_bias[:], router_bias.partition_broadcast(HALF)))
        if hidden is not None:
            w1, b1 = hidden
            loads += [(w1_m[:], w1[0:DM, :]), (w1_t[:], w1[DM:D, :]),
                      (b1_m[:], b1[0:DM].unsqueeze(1)), (b1_t[:], b1[DM:D].unsqueeze(1))]

        @block.sync
        def _(sp):
            for dst, src in loads:
                sp.dma_start(dst, src).then_inc(loaded, 16)
            sp.wait_ge(loaded, 16 * len(loads))

        @block.tensor
        def _(pe):
            pe.wait_ge(loaded, 16 * len(loads))
            if hidden is not None:
                for g in range(4):
                    c = slice(g * PIECE, (g + 1) * PIECE)
                    if g >= 2:
                        pe.wait_ge(hid_kept, 2 * (g - 1))
                    for i, m in enumerate((slice(0, DM), slice(DM, D))):
                        o = hp[0:m.stop - m.start, g % 2, i, 0:PIECE]
                        nc.tensor.matmul(o, w1_m[:, m], x_main[:, c], start=True, stop=False)
                        last = nc.tensor.matmul(o, w1_t[:, m], x_tail[0:DT, c], start=False, stop=True)
                    last.then_inc(hid_done, 1)
                pe.wait_ge(hid_kept, 8)
            xm, xt = (h_main, h_tail) if hidden is not None else (x_main, x_tail)
            for t in range(TILES):
                c = slice(t * HALF, (t + 1) * HALF)
                o = sp_[0:HALF, t * E_NUM:(t + 1) * E_NUM]
                nc.tensor.matmul(o, xm[:, c], rw_m[:], start=True, stop=False)
                last = nc.tensor.matmul(o, xt[0:DT, c], rw_t[:], start=False, stop=True)
            last.then_inc(scored, 1)
            pe.wait_ge(chosen, 1)
            nc.tensor.matmul(cp[0:HALF, 0:TILES * E_NUM], upper[:], both[:].rearrange("p t e -> p (t e)"),
                             start=True, stop=True)
            nc.tensor.matmul(tp[:, 0:TILES * E_NUM].rearrange("p (e t) -> p e t", t=TILES), ones[:],
                             both[:].rearrange("p t e -> p e t"), start=True, stop=True).then_inc(counted, 1)
            pe.wait_ge(spread, 1)
            for k in range(2 * TILES):
                last = nc.tensor.matmul(ip[:, 0:2 * SLOTS], in_row[:, k, :], ids[:, k].rearrange("p a s -> p (a s)"),
                                        start=k == 0, stop=k == 2 * TILES - 1)
            last.then_inc(inverted, 1)

        @block.scalar
        def _(act):
            if hidden is not None:
                act.wait_ge(loaded, 16 * len(loads))
                for g in range(4):
                    c = slice(g * PIECE, (g + 1) * PIECE)
                    act.wait_ge(hid_done, g + 1)
                    nc.scalar.activation(h_main[:, c], hp[:, g % 2, 0, 0:PIECE], ACT.Relu,
                                         bias=b1_m[:, 0:1]).then_inc(hid_kept, 1)
                    nc.scalar.activation(h_tail[:, c], hp[0:DT, g % 2, 1, 0:PIECE], ACT.Relu,
                                         bias=b1_t[:, 0:1]).then_inc(hid_kept, 1)
            act.wait_ge(margin, 1)
            nc.scalar.activation(best[:, 2, :], best[:, 2, :], ACT.Exp).then_inc(raised, 1)

        @block.vector
        def _(dve):
            V = nc.vector
            link = chained(dve, seq)

            def wide(x, n=E_NUM):
                return x.unsqueeze(2).broadcast_to([x.shape[0], x.shape[1], n])

            V.memset(ones[:], 1.0)
            V.memset(e_ones[:], 1.0)
            link(V.tensor_copy(upper[:], view["upper"][0:HALF, :]))
            dve.wait_ge(loaded, 16 * len(loads))
            dve.wait_ge(scored, 1)
            s3 = sp_[0:HALF, 0:TILES * E_NUM].rearrange("p (t e) -> p t e", e=E_NUM)
            rank = view["rank"][0:HALF].unsqueeze(1).broadcast_to(TE)
            if router_bias is None:
                link(V.tensor_copy(score[:], s3))
            else:
                link(V.tensor_tensor(score[:], s3, r_bias[:].unsqueeze(1).broadcast_to(TE), ALU.add))

            def top(values, peak, onehot):
                link(V.tensor_reduce(peak, values[:], AX.X, ALU.max))
                link(V.tensor_tensor(key[:], values[:], wide(peak), ALU.is_ge))
                link(V.tensor_tensor(key[:], key[:], rank, ALU.mult))
                link(V.tensor_reduce(best[:, 3, :], key[:], AX.X, ALU.max))
                link(V.tensor_tensor(onehot[:], key[:], wide(best[:, 3, :]), ALU.is_equal))

            top(score, best[:, 0, :], first)
            link(V.scalar_tensor_tensor(out=score2[:], in0=first[:], scalar=-1e30, in1=score[:],
                                        op0=ALU.mult, op1=ALU.add))
            top(score2, best[:, 1, :], second)
            V.tensor_tensor(both[:], first[:], second[:], ALU.add).then_inc(chosen, 1)
            V.tensor_tensor(best[:, 2, :], best[:, 1, :], best[:, 0, :], ALU.subtract).then_inc(margin, 1)
            dve.wait_ge(counted, 1)
            link(V.tensor_copy(totals[:], tp[:, 0:TILES * E_NUM].rearrange("p (e t) -> p e t", t=TILES)))
            flat = lambda x: x[:].rearrange("p a b -> p (a b)")
            link(V.tensor_tensor_scan(flat(running), view["within"], flat(totals), 0.0, ALU.mult, ALU.add))
            cnt = running[:, :, TILES - 1]
            link(V.tensor_tensor(over[:], wide(cnt, 11), view["steps"].unsqueeze(1).broadcast_to([P, E_NUM, 11]),
                                 ALU.is_gt))
            link(V.tensor_reduce(e_tiles[:], over[:], AX.X, ALU.add))
            link(V.tensor_tensor_scan(e_end[:], e_ones[:], e_tiles[:], 0.0, ALU.mult, ALU.add))
            link(V.tensor_tensor(e_start[:], e_end[:], e_tiles[:], ALU.subtract))
            link(V.tensor_tensor(running[:], running[:], totals[:], ALU.subtract))
            link(V.scalar_tensor_tensor(out=running[:], in0=wide(e_start[:], TILES), scalar=float(P),
                                        in1=running[:], op0=ALU.mult, op1=ALU.add))
            link(V.tensor_tensor(pos[:], running[0:HALF].rearrange("p e t -> p t e"),
                                 cp[0:HALF, 0:TILES * E_NUM].rearrange("p (t e) -> p t e", e=E_NUM), ALU.add))
            for k, onehot in enumerate((first, second)):
                link(V.tensor_tensor(key[:], onehot[:], pos[:], ALU.mult))
                link(V.tensor_reduce(slot_f[:, k, :], key[:], AX.X, ALU.add))
            link(V.tensor_copy(pair_slot[:], slot_f[:]))
            link(V.tensor_single_scalar(slot_hi[:], pair_slot[:], 7, ALU.arith_shift_right))
            link(V.tensor_single_scalar(slot_lo[:], pair_slot[:], P - 1, ALU.bitwise_and))
            link(V.tensor_copy(hi_f[:], slot_hi[:].rearrange("p k t -> p (k t)")))
            link(V.tensor_copy(lo_f[:], slot_lo[:].rearrange("p k t -> p (k t)")))
            link(V.tensor_tensor(in_tile[:], wide(hi_f[:], SLOTS),
                                 view["count"][0:HALF, 0:SLOTS].unsqueeze(1).broadcast_to([HALF, 2 * TILES, SLOTS]),
                                 ALU.is_equal))
            link(V.tensor_tensor(in_row[:], wide(lo_f[:], P),
                                 view["count"][0:HALF].unsqueeze(1).broadcast_to([HALF, 2 * TILES, P]), ALU.is_equal))
            for k in range(2):
                part = slice(k * TILES, (k + 1) * TILES)
                link(V.tensor_tensor(ids[:, part, 0, :], in_tile[:, part, :], wide(view["tile"][0:HALF], SLOTS),
                                     ALU.mult))
            V.tensor_scalar(ids[:, :, 1, :], in_tile[:], view["row"][0:HALF, 0:1], None, ALU.mult).then_inc(spread, 1)
            link(V.tensor_tensor(passed[:], e_end[:].unsqueeze(1).broadcast_to([P, SLOTS, E_NUM]),
                                 wide(view["count"][:, 0:SLOTS]), ALU.is_le))
            link(V.tensor_reduce(passed_n[:], passed[:], AX.X, ALU.add))
            link(V.tensor_scalar(passed_n[:], passed_n[:], float(E_NUM - 1), None, ALU.min))
            V.tensor_copy(slot_expert[:], passed_n[:])
            dve.wait_ge(raised, 1)
            link(V.tensor_scalar(best[:, 3, :], best[:, 2, :], 1.0, None, ALU.add))
            link(V.reciprocal(gate_w[:, 0, :], best[:, 3, :]))
            link(V.tensor_tensor(gate_w[:, 1, :], gate_w[:, 0, :], best[:, 2, :], ALU.mult))
            dve.wait_ge(inverted, 1)
            link(V.tensor_copy(token_hi[:], ip[:, SLOTS:2 * SLOTS]))
            link(V.scalar_tensor_tensor(out=token_f[:], in0=ip[:, 0:SLOTS], scalar=float(HALF), in1=token_hi[:],
                                        op0=ALU.mult, op1=ALU.add))
            link(V.tensor_copy(slot_token[:], token_f[:]))


def experts(nc, name, h, wt, n_up, ident, x_rows, y_rows, up_bias, down_bias, gate_w, pair_slot, slot_token,
            slot_expert):
    gated = n_up == 2
    up = n_up * FF
    HF = FF // 2
    NC = FF // P
    UN = 1.0 / W_SCALE
    with ExitStack() as ctx:
        def sb(s, shape, dt=F32):
            return ctx.enter_context(nc.sbuf_tensor(f"{name}_{s}", shape, dt))

        def ps(s, shape):
            return ctx.enter_context(nc.psum_tensor(f"{name}_{s}", shape, F32))

        stage_sem = stage_semaphores(nc, ctx)

        def sem(s):
            return stage_sem(f"{name}_{s}")

        xg = sb("xg", [P, 4, XROW])
        xh = sb("xh", [P, 2, 2, P], F16)
        xl = sb("xl", [P, 2, 2, P], F16)
        sg = sb("sg", [P, 2, HF]) if gated else None
        m = sb("m", [P, 2, HF])
        mh = sb("mh", [P, 2, FF], F16)
        ml = sb("ml", [P, 2, FF], F16)
        yt = sb("yt", [P, D])
        y = sb("y", [P, 2, D])
        yg = sb("yg", [HALF, 2, TILES, D])
        if not gated:
            b_up = sb("b_up", [P, E_NUM, FF])
            b_down = sb("b_down", [P, E_NUM, D])
        up_ps = [[ps(f"up{n}{a}", [P, 512]) for a in range(2)] for n in range(n_up)]
        mt_ps = [ps(f"mt{a}", [P, 512]) for a in range(2)]
        y_ps = ps("y_ps", [P, 512])
        xt_ps = ps("xt_ps", [P, 512])

        bias_in = sem("bias_in")
        fetched = [sem(f"fetched{i}") for i in range(4)]
        x_turned = sem("x_turned")
        x_high = sem("x_high")
        x_split = sem("x_split")
        up_done = sem("up_done")
        lit = sem("lit")
        m_ready = sem("m_ready")
        m_turned = sem("m_turned")
        m_high = sem("m_high")
        m_split = sem("m_split")
        down_done = sem("down_done")
        half_sum = sem("half_sum")
        y_ready = sem("y_ready")
        y_out = [sem("y_out0"), sem("y_out1")]
        y_back = [sem(f"y_back{t}") for t in range(TILES // 4)]
        summed = sem("summed")
        block = ctx.enter_context(nc.Block())

        def all_steps(eng, step):
            for j in range(4):
                step(0, j)
            with eng.Fori(1, SLOTS // 4 - 1) as k:
                for j in range(4):
                    step(k, j)
            for j in range(4):
                step(SLOTS // 4 - 1, j)

        def is_first(k, j):
            return isinstance(k, int) and k == 0 and j == 0

        def is_last(k, j):
            return isinstance(k, int) and k == SLOTS // 4 - 1 and j == 3

        def early(k, j, n):
            return isinstance(k, int) and k == 0 and j < n

        def expert_of(eng, i):
            return eng.value_load(slot_expert[0:1, bass.ds(i, 1)], min_val=0, max_val=E_NUM - 1)

        @block.sync
        def _(sp):
            if not gated:
                sp.dma_start(b_up[:].rearrange("p e f -> p (e f)"), up_bias.partition_broadcast(P)).then_inc(bias_in, 16)
                sp.dma_start(b_down[:].rearrange("p e f -> p (e f)"),
                             down_bias.partition_broadcast(P)).then_inc(bias_in, 16)

            def step(k, j):
                i = 4 * k + j
                sp.wait_ge(y_ready, i + 1)
                sp.dma_start(y_rows[bass.ds(i * P, P), :], y[:, j % 2, :]).then_inc(y_out[j % 2], 16)
            all_steps(sp, step)
            for a in range(2):
                sp.wait_ge(y_out[a], 16 * SLOTS // 2)

        @block.gpsimd
        def _(pool):
            for i in range(SLOTS):
                if i >= 4:
                    pool.wait_ge(x_turned, i - 3)
                nc.gpsimd.indirect_dma_start(xg[:, i % 4, :], None, x_rows, bass.IndirectOffsetOnAxis(
                    ap=slot_token[:, i:i + 1].bitcast(U32), axis=0)).then_inc(fetched[i % 4], 16)
            for a in range(2):
                pool.wait_ge(y_out[a], 16 * SLOTS // 2)
            for t in range(TILES):
                for c in range(2):
                    nc.gpsimd.indirect_dma_start(yg[:, c, t, :], None, y_rows, bass.IndirectOffsetOnAxis(
                        ap=pair_slot[:, c, t:t + 1].bitcast(U32), axis=0)).then_inc(y_back[t // 4], 16)

        @block.tensor
        def _(pe):
            def turn_x(k, j, i):
                pe.wait_ge(fetched[j], 16 * k + 16)
                nc.tensor.transpose(xt_ps[:, 0:P], xg[:, j, 0:P], ident[:])
                nc.tensor.transpose(xt_ps[:, P:2 * P], xg[:, j, P:2 * P], ident[:]).then_inc(x_turned, 1)

            def up_half(e, s, a, i):
                for n in range(n_up):
                    o = up_ps[n][a][:, 0:HF]
                    c = n * FF + a * HF
                    high, tail, low = (wt[:, bass.ds(e, 1), f + c:f + c + HF].rearrange("p a f -> p (a f)")
                                       for f in (0, up, 2 * up))
                    nc.tensor.matmul(o, xh[:, s, 0], high, start=True, stop=False)
                    nc.tensor.matmul(o, xl[:, s, 0], high, start=False, stop=False)
                    nc.tensor.matmul(o, xh[:, s, 0], low, start=False, stop=False)
                    nc.tensor.matmul(o, xh[:, s, 1], tail, start=False, stop=False)
                    last = nc.tensor.matmul(o, xl[:, s, 1], tail, start=False, stop=True)
                last.then_inc(up_done, 1)

            def down(i, s, wait_bank):
                e = expert_of(pe, i)
                if wait_bank:
                    pe.wait_ge(y_ready, i)
                pe.wait_ge(m_split, 2 * i + 2)
                for c in range(NC):
                    w = wt[:, bass.ds(e, 1), 3 * up + 2 * D * c:3 * up + 2 * D * (c + 1)].rearrange("p a f -> p (a f)")
                    wh = wt[:, bass.ds(e, 1), 3 * up + 2 * D * c:3 * up + 2 * D * c + D].rearrange("p a f -> p (a f)")
                    nc.tensor.matmul(y_ps[:, 0:2 * D], mh[:, s, c * P:(c + 1) * P], w, start=c == 0, stop=False)
                    last = nc.tensor.matmul(y_ps[:, D:2 * D], ml[:, s, c * P:(c + 1) * P], wh, start=False,
                                            stop=c == NC - 1)
                last.then_inc(down_done, 1)

            def step(k, j):
                i, s = 4 * k + j, j % 2
                if not is_last(k, j):
                    pe.wait_ge(x_split, i + 1)
                    turn_x(k + (j + 1) // 4, (j + 1) % 4, i + 1)
                e = expert_of(pe, i)
                pe.wait_ge(x_split, i + 1)
                for a in range(2):
                    if not is_first(k, j):
                        pe.wait_ge(m_ready, 2 * i - 1 + a)
                    up_half(e, s, a, i)
                if not is_first(k, j):
                    down(i - 1, 1 - s, not early(k, j, 2))
                for a in range(2):
                    pe.wait_ge(m_ready, 2 * i + a + 1)
                    for c in range(3):
                        last = nc.tensor.transpose(mt_ps[a][:, c * P:(c + 1) * P], m[:, a, c * P:(c + 1) * P], ident[:])
                    last.then_inc(m_turned, 1)
            turn_x(0, 0, 0)
            all_steps(pe, step)
            down(SLOTS - 1, 1, True)

        @block.scalar
        def _(act):
            def split_x(s, i, wait_slot):
                act.wait_ge(x_turned, i + 1)
                if wait_slot:
                    act.wait_ge(up_done, 2 * i - 2)
                nc.scalar.activation(xh[:, s].rearrange("p a t -> p (a t)"), xt_ps[:, 0:2 * P],
                                     ACT.Copy).then_inc(x_high, 1)

            def step(k, j):
                i, s = 4 * k + j, j % 2
                if not is_last(k, j):
                    split_x(1 - s, i + 1, not early(k, j, 1))
                if gated:
                    for a in range(2):
                        act.wait_ge(up_done, 2 * i + a + 1)
                        if not is_first(k, j):
                            act.wait_ge(m_ready, 2 * i + a - 1)
                        nc.scalar.activation(sg[:, a, :], up_ps[0][a][:, 0:HF], ACT.Silu, scale=UN).then_inc(lit, 1)
                for a in range(2):
                    act.wait_ge(m_turned, 2 * i + a + 1)
                    if not early(k, j, 2):
                        act.wait_ge(down_done, i - 1)
                    nc.scalar.activation(mh[:, s, a * HF:(a + 1) * HF], mt_ps[a][:, 0:HF],
                                         ACT.Copy if gated else ACT.Relu).then_inc(m_high, 1)
            split_x(0, 0, False)
            all_steps(act, step)

        @block.vector
        def _(dve):
            def low_x(s, i):
                dve.wait_ge(x_high, i + 1)
                nc.vector.tensor_tensor(xl[:, s].rearrange("p a t -> p (a t)"), xt_ps[:, 0:2 * P],
                                        xh[:, s].rearrange("p a t -> p (a t)"), ALU.subtract).then_inc(x_split, 1)

            def finish(i, s, wait_out, turn):
                e = None if gated else expert_of(dve, i)
                dve.wait_ge(down_done, i + 1)
                if gated:
                    nc.vector.tensor_scalar(yt[:], y_ps[:, 0:D], UN, None, ALU.mult).then_inc(half_sum, 1)
                else:
                    nc.vector.scalar_tensor_tensor(
                        out=yt[:], in0=y_ps[:, 0:D], scalar=UN, in1=b_down[:, bass.ds(e, 1), :].rearrange("p a f -> p (a f)"),
                        op0=ALU.mult, op1=ALU.add).then_inc(half_sum, 1)
                dve.wait_ge(half_sum, i + 1)
                if wait_out:
                    dve.wait_ge(y_out[s], turn)
                nc.vector.scalar_tensor_tensor(out=y[:, s, :], in0=y_ps[:, D:2 * D], scalar=UN, in1=yt[:],
                                               op0=ALU.mult, op1=ALU.add).then_inc(y_ready, 1)

            def step(k, j):
                i, s = 4 * k + j, j % 2
                if not is_last(k, j):
                    low_x(1 - s, i + 1)
                if not gated:
                    e = expert_of(dve, i)
                for a in range(2):
                    if not is_first(k, j):
                        dve.wait_ge(m_turned, 2 * i + a - 1)
                    if gated:
                        dve.wait_ge(lit, 2 * i + a + 1)
                        nc.vector.scalar_tensor_tensor(out=m[:, a, :], in0=up_ps[1][a][:, 0:HF], scalar=UN,
                                                       in1=sg[:, a, :], op0=ALU.mult,
                                                       op1=ALU.mult).then_inc(m_ready, 1)
                    else:
                        dve.wait_ge(up_done, 2 * i + a + 1)
                        bias = b_up[:, bass.ds(e, 1), a * HF:(a + 1) * HF].rearrange("p a f -> p (a f)")
                        nc.vector.scalar_tensor_tensor(out=m[:, a, :], in0=up_ps[0][a][:, 0:HF], scalar=UN, in1=bias,
                                                       op0=ALU.mult, op1=ALU.add).then_inc(m_ready, 1)
                if not is_first(k, j):
                    finish(i - 1, 1 - s, not early(k, j, 3), 32 * k + 16 * ((j + 3) // 2) - 32)
                for a in range(2):
                    dve.wait_ge(m_high, 2 * i + a + 1)
                    out, hi, full = ml[:, s, a * HF:(a + 1) * HF], mh[:, s, a * HF:(a + 1) * HF], mt_ps[a][:, 0:HF]
                    if gated:
                        ins = nc.vector.tensor_tensor(out, full, hi, ALU.subtract)
                    else:
                        ins = nc.vector.scalar_tensor_tensor(out=out, in0=full, scalar=0.0, in1=hi, op0=ALU.max,
                                                             op1=ALU.subtract)
                    ins.then_inc(m_split, 1)
            if not gated:
                dve.wait_ge(bias_in, 32)
            low_x(0, 0)
            all_steps(dve, step)
            finish(SLOTS - 1, 1, True, 16 * ((SLOTS - 1) // 2))
            for t in range(TILES):
                if t % 4 == 0:
                    dve.wait_ge(y_back[t // 4], 4 * 32)
                for c in range(2):
                    nc.vector.scalar_tensor_tensor(out=h[:, t, :], in0=yg[:, c, t, :], scalar=gate_w[:, c, t:t + 1],
                                                   in1=h[:, t, :], op0=ALU.mult, op1=ALU.add).then_inc(summed, 1)
                    dve.wait_ge(summed, 2 * t + c + 1)


HEADS = 12
HD = D // HEADS
GROUP = 32
MT = HEADS * GROUP // P
BANK = 64
KEYS = SEQ + BANK
KT = KEYS // 2
OWN = SEQ - KT


def attention(nc, h, x_main, x_tail, ident, wqk, bqk, wv, bv, bank_kT, bank_v):
    MAXES = 2 * MT
    with ExitStack() as ctx:
        def sb(s, shape, dt=F32):
            return ctx.enter_context(nc.sbuf_tensor(f"at_{s}", shape, dt))

        def ps(s, shape):
            return ctx.enter_context(nc.psum_tensor(f"at_{s}", shape, F32))

        stage_sem = stage_semaphores(nc, ctx)

        def sem(s):
            return stage_sem(f"at_{s}")

        w_m = sb("wqk_main", [P, 2 * MT, P])
        w_t = sb("wqk_tail", [DT, 2 * MT, P])
        b_qk = sb("bqk", [P, 2 * MT])
        wv_m = sb("wv_main", [P, D])
        wv_t = sb("wv_tail", [DT, D])
        b_v = sb("b_v", [P, D])
        xb_m = sb("xb_main", [P, SEQ])
        xb_t = sb("xb_tail", [DT, SEQ])
        q = [sb(f"q{s}", [P, MT, SEQ]) for s in range(2)]
        k_ = [sb(f"k{s}", [P, MT, KEYS]) for s in range(2)]
        q16 = sb("q16", [P, MT, SEQ], F16)
        k16 = sb("k16", [P, MT, KEYS], F16)
        v = [sb(f"v{s}", [KT, 2, HEADS, HD + 1]) for s in range(2)]
        shift = sb("shift", [HALF, MAXES, P])
        e = sb("e", [KT, 2, 2, SEQ])
        rden = sb("rden", [HALF, 2, HEADS])
        att = sb("att", [HALF, 2, D])
        work = ps("work", [P, 4, 512])
        st = [ps(f"st{s}", [P, 512]) for s in range(2)]
        o = [ps(f"o{s}", [P, 512]) for s in range(2)]

        loaded = sem("loaded")
        preset = sem("preset")
        x_copied = sem("x_copied")
        projected = sem("projected")
        qk_kept = sem("qk_kept")
        k_halved = sem("k_halved")
        v_kept = sem("v_kept")
        scored = sem("scored")
        peaked = sem("peaked")
        peaks_turned = sem("peaks_turned")
        shifted = sem("shifted")
        st_ready = sem("st_ready")
        raised = sem("raised")
        mixed = sem("mixed")
        seq = sem("dve_seq")
        added = sem("added")
        LOADS = 16 * (6 + 2 * (MT + HEADS))
        block = ctx.enter_context(nc.Block())
        QK = slice(0, MT * SEQ)

        def all_rows(eng, step):
            with eng.Fori(0, BATCH // 2 - 1) as k:
                for s in range(2):
                    step(2 * k + s, s, True)
            for s in range(2):
                step(BATCH - 2 + s, s, s == 0)

        @block.sync
        def _(sp):
            for dst, src in ((w_m[:], wqk[0:DM]), (w_t[:], wqk[DM:D]), (b_qk[:], bqk), (wv_m[:], wv[0:DM, :]),
                             (wv_t[:], wv[DM:D, :]), (b_v[:], bv.partition_broadcast(P))):
                sp.dma_start(dst, src).then_inc(loaded, 16)
            for s in range(2):
                for m in range(MT):
                    sp.dma_start(k_[s][:, m, SEQ:KEYS], bank_kT[:, m, :]).then_inc(loaded, 16)
                for n in range(HEADS):
                    sp.dma_start(v[s][OWN:KT, 1, n, 0:HD], bank_v[:, n * HD:(n + 1) * HD]).then_inc(loaded, 16)
            sp.wait_ge(loaded, LOADS)

        @block.gpsimd
        def _(pool):
            nc.gpsimd.memset(shift[:], 0.0).then_inc(preset, 1)
            for s in range(2):
                nc.gpsimd.memset(v[s][:, :, :, HD:HD + 1], 1.0).then_inc(preset, 1)

        @block.tensor
        def _(pe):
            def project(b, part):
                if part == 0:
                    pe.wait_ge(x_copied, 2 * b + 2)
                    pe.wait_ge(peaked, MAXES * b)
                    pe.wait_ge(shifted, b)
                if part < 2:
                    for m in range(MT):
                        out = work[:, part, m * SEQ:(m + 1) * SEQ]
                        nc.tensor.matmul(out, w_m[:, part * MT + m, :], xb_m[:], start=True, stop=False)
                        last = nc.tensor.matmul(out, w_t[:, part * MT + m, :], xb_t[:], start=False, stop=True)
                else:
                    for t, (lo, hi) in enumerate(((0, KT), (KT, SEQ))):
                        out = work[0:hi - lo, 2, t * D:(t + 1) * D]
                        nc.tensor.matmul(out, xb_m[:, lo:hi], wv_m[:], start=True, stop=False)
                        last = nc.tensor.matmul(out, xb_t[:, lo:hi], wv_t[:], start=False, stop=True)
                last.then_inc(projected, 1)

            def score(b, g):
                half, m = divmod(g, MT)
                if g == 0:
                    pe.wait_ge(k_halved, 2 * b + 2)
                    pe.wait_ge(v_kept, 2 * b + 2)
                else:
                    pe.wait_ge(peaked, MAXES * b + g)
                for r in range(4):
                    rows = slice(r * GROUP, (r + 1) * GROUP)
                    last = nc.tensor.matmul(work[0:HALF, r, 0:KEYS], q16[rows, m, half * HALF:(half + 1) * HALF],
                                            k16[rows, m, :], start=True, stop=True)
                last.then_inc(scored, 1)

            def turn_peaks(b):
                pe.wait_ge(peaked, MAXES * b + MAXES)
                for g in range(MAXES):
                    half, m = divmod(g, MT)
                    c = m * SEQ + half * HALF
                    last = nc.tensor.transpose(work[:, 3, c:c + HALF], shift[:, g, :], ident[0:HALF, 0:HALF])
                last.then_inc(peaks_turned, 1)

            def score_turned(s, n):
                m, r = divmod(n, 4)
                rows = slice(r * GROUP, (r + 1) * GROUP)
                for t in range(2):
                    last = nc.tensor.matmul(st[n % 2][0:KT, t * SEQ:(t + 1) * SEQ], k_[s][rows, m, t * KT:(t + 1) * KT],
                                            q[s][rows, m, :], start=True, stop=True)
                last.then_inc(st_ready, 1)

            def mix(b, s, n):
                pe.wait_ge(raised, HEADS * b + n + 1)
                for half in range(2):
                    c = (half * HEADS + n) * (HD + 1)
                    for t in range(2):
                        last = nc.tensor.matmul(o[s][0:HALF, c:c + HD + 1], e[:, n % 2, t, half * HALF:(half + 1) * HALF],
                                                v[s][:, t, n, :], start=t == 0, stop=t == 1)
                return last

            def prepare(b, part):
                if part < 3:
                    project(b, part)
                elif part < 3 + MAXES:
                    score(b, part - 3)
                elif part == 3 + MAXES:
                    turn_peaks(b)

            def step(b, s, more):
                for n in range(HEADS):
                    if n + 1 < HEADS:
                        score_turned(s, n + 1)
                    elif more:
                        pe.wait_ge(shifted, b + 2)
                        score_turned(1 - s, 0)
                    if more:
                        prepare(b + 1, n)
                    last = mix(b, s, n)
                last.then_inc(mixed, 1)

            pe.wait_ge(loaded, LOADS)
            for part in range(4 + MAXES):
                prepare(0, part)
            pe.wait_ge(shifted, 1)
            pe.wait_ge(preset, 3)
            score_turned(0, 0)
            all_rows(pe, step)

        @block.scalar
        def _(act):
            def copy_x(b):
                act.wait_ge(projected, 3 * b)
                nc.scalar.activation(xb_m[:], x_main[:, bass.ds(b * SEQ, SEQ)], ACT.Copy).then_inc(x_copied, 1)
                nc.scalar.activation(xb_t[:], x_tail[:, bass.ds(b * SEQ, SEQ)], ACT.Copy).then_inc(x_copied, 1)

            def keep(b, s, part):
                act.wait_ge(projected, 3 * b + part + 1)
                for m in range(MT):
                    nc.scalar.activation((q, k_)[part][s][:, m, 0:SEQ], work[:, part, m * SEQ:(m + 1) * SEQ],
                                         ACT.Identity, bias=b_qk[:, part * MT + m:part * MT + m + 1]).then_inc(qk_kept, 1)

            def step(b, s, more):
                if more:
                    copy_x(b + 1)
                for n in range(HEADS):
                    act.wait_ge(st_ready, HEADS * b + n + 1)
                    nc.scalar.activation(e[:, n % 2].rearrange("p t c -> p (t c)"), st[n % 2][0:KT, 0:2 * SEQ], ACT.Exp,
                                         scale=float(HD) ** -0.5).then_inc(raised, 1)
                    if more and n < 2:
                        keep(b + 1, 1 - s, n)

            act.wait_ge(loaded, LOADS)
            nc.scalar.activation(xb_m[:], x_main[:, 0:SEQ], ACT.Copy).then_inc(x_copied, 1)
            nc.scalar.activation(xb_t[:], x_tail[:, 0:SEQ], ACT.Copy).then_inc(x_copied, 1)
            keep(0, 0, 0)
            keep(0, 0, 1)
            all_rows(act, step)

        @block.vector
        def _(dve):
            def prepare(b, s):
                dve.wait_ge(projected, 3 * b + 3)
                for t, n in ((0, KT), (1, OWN)):
                    nc.vector.tensor_tensor(v[s][0:n, t, :, 0:HD], work[0:n, 2, t * D:(t + 1) * D].rearrange(
                        "p (n c) -> p n c", c=HD), b_v[0:n].rearrange("p (n c) -> p n c", c=HD), ALU.add).then_inc(v_kept, 1)
                for part, (half, full, n) in enumerate(((q16, q, SEQ), (k16, k_, KEYS))):
                    dve.wait_ge(qk_kept, 2 * MT * b + MT * (part + 1))
                    nc.vector.tensor_copy(half[:], full[s][:]).then_inc(k_halved, 1)
                for g in range(MAXES):
                    dve.wait_ge(scored, MAXES * b + g + 1)
                    nc.vector.tensor_reduce(shift[:, g, HD::GROUP], work[0:HALF, :, 0:KEYS], AX.X, ALU.max,
                                            negate=True).then_inc(peaked, 1)
                dve.wait_ge(peaks_turned, b + 1)
                q2 = q[s][:].rearrange("p m c -> p (m c)")
                nc.vector.tensor_tensor(q2, q2, work[:, 3, QK], ALU.add).then_inc(shifted, 1)

            def step(b, s, more):
                if more:
                    prepare(b + 1, 1 - s)
                dve.wait_ge(mixed, b + 1)
                out = o[s][0:HALF, 0:2 * HEADS * (HD + 1)].rearrange("p (a n c) -> p a n c", a=2, c=HD + 1)
                nc.vector.reciprocal(rden[:].unsqueeze(3), out[:, :, :, HD:HD + 1]).then_inc(seq, 1)
                dve.wait_ge(seq, 3 * b + 1)
                for half in range(2):
                    nc.vector.tensor_tensor(att[:, half, :].rearrange("p (n c) -> p n c", c=HD), out[:, half, :, 0:HD],
                                            rden[:, half, :].unsqueeze(2).broadcast_to([HALF, HEADS, HD]),
                                            ALU.mult).then_inc(seq, 1)
                dve.wait_ge(seq, 3 * b + 3)
                hb = h[:, bass.ds(2 * b, 2), :]
                nc.vector.tensor_tensor(hb, hb, att[:], ALU.add).then_inc(added, 1)

            dve.wait_ge(preset, 3)
            dve.wait_ge(loaded, LOADS)
            prepare(0, 0)
            all_rows(dve, step)


def program(nc, a):
    with ExitStack() as ctx:
        def sb(name, shape, dt=F32):
            return ctx.enter_context(nc.sbuf_tensor(name, shape, dt))

        h = sb("h", [HALF, TILES, D])
        ident = sb("ident", [P, P])
        neg_half = sb("neg_half", [P, TILES])
        xn = sb("xn", [HALF, TILES, XROW])
        consts = sb("consts", [P, sum(CONSTS.values())])
        gate_w = sb("gate_w", [HALF, 2, TILES])
        pair_slot = sb("pair_slot", [HALF, 2, TILES], I32)
        slot_token = sb("slot_token", [P, SLOTS], I32)
        slot_expert = sb("slot_expert", [P, SLOTS], I32)
        x_rows = nc.dram_tensor("x_rows", [TOKENS, XROW], F32, kind="Internal").ap()
        y_rows = nc.dram_tensor("y_rows", [SLOT_ROWS, D], F32, kind="Internal").ap()
        flat = lambda v: v.rearrange("e f -> (e f)")

        tokenizer(nc, a["patches"], a["L0_tok_w"], a["L0_tok_ln_gamma"], a["L0_tok_ln_beta"], a["L0_tok_b"],
                  a["txt"], a["consts"], ident, neg_half, consts, h)
        with ExitStack() as c2:
            xd = c2.enter_context(nc.sbuf_tensor("xd", [P, UNITS * UCOLS], F32))
            normalize(nc, "ln0", h, xn, ident, neg_half, xd[:, 0:2 * UCOLS], xd[:, 2 * UCOLS:], True)
            state_scan(nc, h, xd, ident, a["L0_attn_W_bc"], a["L0_attn_W_dt"], a["L0_attn_W_dtp"],
                       (a["L0_attn_b_dt"], a["L0_attn_rms_scale"], a["L0_attn_D_param"]), a["L0_attn_A_log"])
        x_main = sb("x_main", [P, TOKENS])
        x_tail = sb("x_tail", [DT, TOKENS])
        with ExitStack() as c2:
            wt = c2.enter_context(nc.sbuf_tensor("wt0", [P, E_NUM, 3 * FF + 2 * FF // P * D], F16))
            split_weights(nc, "w0", a["packed0"], wt, 1)
            normalize(nc, "ln1", h, xn, ident, neg_half, x_main, x_tail, False, x_rows)
            route(nc, "r0", x_main, x_tail, consts, (a["Wr1T"], a["L0_ffn_br1"]), a["Wr2T"], a["L0_ffn_br2"],
                  gate_w, pair_slot, slot_token, slot_expert)
            experts(nc, "e0", h, wt, 1, ident, x_rows, y_rows, flat(a["L0_ffn_b1"]), flat(a["L0_ffn_b2"]),
                    gate_w, pair_slot, slot_token, slot_expert)
        normalize(nc, "ln2", h, xn, ident, neg_half, x_main, x_tail, False)
        attention(nc, h, x_main, x_tail, ident, a["wqk"], a["bqk"], a["wvT"], a["bv"], a["bank_kT"],
                  a["L1_attn_bank_v"])
        with ExitStack() as c2:
            wt = c2.enter_context(nc.sbuf_tensor("wt1", [P, E_NUM, 6 * FF + 2 * FF // P * D], F16))
            split_weights(nc, "w1", a["packed1"], wt, 2)
            normalize(nc, "ln3", h, xn, ident, neg_half, x_main, x_tail, False, x_rows)
            route(nc, "r1", x_main, x_tail, consts, None, a["router_wT"], None,
                  gate_w, pair_slot, slot_token, slot_expert)
            experts(nc, "e1", h, wt, 2, ident, x_rows, y_rows, None, None,
                    gate_w, pair_slot, slot_token, slot_expert)
        stored = ctx.enter_context(nc.semaphore("out_stored"))
        block = ctx.enter_context(nc.Block())

        @block.sync
        def _(sp):
            sp.dma_start(a["out"].rearrange("b (s p) d -> p (b s) d", p=HALF), h[:]).then_inc(stored, 16)
            sp.wait_ge(stored, 16)


def laid_out(inputs):
    import numpy as np
    a = {k: np.ascontiguousarray(v) for k, v in inputs.items()}
    x = a.pop("x")
    B, C, H, W = x.shape
    p = 16
    shifts = np.zeros((5, B, C, H, W), x.dtype)
    shifts[0] = x
    shifts[1, :, :, :, 1:] = x[:, :, :, :-1]
    shifts[2, :, :, :, :-1] = x[:, :, :, 1:]
    shifts[3, :, :, 1:, :] = x[:, :, :-1, :]
    shifts[4, :, :, :-1, :] = x[:, :, 1:, :]
    t = shifts.reshape(5, B, C, H // p, p, W // p, p).transpose(4, 6, 0, 2, 1, 3, 5)
    a["patches"] = np.ascontiguousarray(t).reshape(p * p * 5 * C, B * (H // p) * (W // p))

    def pack(ups, down):
        ups = [np.swapaxes(u, 1, 2) for u in ups]
        main = [u[:, :DM] for u in ups]
        tail = [np.concatenate([u[:, DM:], u[:, DM:]], axis=1) for u in ups]
        dn = np.swapaxes(down, 1, 2).reshape(E_NUM, FF // P, P, D).transpose(0, 2, 1, 3).reshape(E_NUM, P, -1)
        return np.ascontiguousarray(np.concatenate(main + tail + [dn], axis=2))

    a["packed0"] = pack([a.pop("L0_ffn_W1")], a.pop("L0_ffn_W2"))
    a["packed1"] = pack([a.pop("L1_ffn_Wg"), a.pop("L1_ffn_Wu")], a.pop("L1_ffn_Wd"))
    a["Wr1T"] = np.ascontiguousarray(a.pop("L0_ffn_Wr1").T)
    a["Wr2T"] = np.ascontiguousarray(a.pop("L0_ffn_Wr2").T)
    a["router_wT"] = np.ascontiguousarray(a.pop("L1_ffn_router_w").T)
    qkv_w, qkv_b = a.pop("L1_attn_qkv_w"), a.pop("L1_attn_qkv_b")
    wqk = np.zeros((D, 2, HEADS, GROUP), qkv_w.dtype)
    bqk = np.zeros((2, HEADS, GROUP), qkv_b.dtype)
    bank = np.zeros((HEADS, GROUP, BANK), qkv_w.dtype)
    wqk[..., :HD] = qkv_w[:2 * D].T.reshape(D, 2, HEADS, HD)
    bqk[..., :HD] = qkv_b[:2 * D].reshape(2, HEADS, HD)
    bank[:, :HD] = a.pop("L1_attn_bank_k").T.reshape(HEADS, HD, BANK)
    bqk[1, :, HD] = 1.0
    bank[:, HD] = 1.0
    a["wqk"] = wqk.reshape(D, 2 * MT, P)
    a["bqk"] = np.ascontiguousarray(bqk.reshape(2 * MT, P).T)
    a["bank_kT"] = np.ascontiguousarray(bank.reshape(MT, P, BANK).transpose(1, 0, 2))
    a["wvT"] = np.ascontiguousarray(qkv_w[2 * D:].T)
    a["bv"] = qkv_b[2 * D:].copy()
    a["consts"] = const_table()
    return a


def kernel(**inputs):
    import numpy as np
    import concourse.bacc as bacc
    from concourse.bass_utils import run_bass_kernel_spmd

    nc = bacc.Bacc("TRN2", target_bir_lowering=False, num_devices=1)
    arrays = {f"in_{k}": v for k, v in laid_out(inputs).items()}
    args = {k[3:]: nc.dram_tensor(k, v.shape, mybir.dt.from_np(v.dtype), kind="ExternalInput").ap()
            for k, v in arrays.items()}
    args["out"] = nc.dram_tensor("out", (BATCH, SEQ, D), F32, kind="ExternalOutput").ap()
    program(nc, args)
    r = run_bass_kernel_spmd(nc, [arrays], core_ids=[0])
    return r.results[0]["out"]
```
